# Optimizing a Trainium2 kernel written in Bass

```python
import numpy as np
import jax
import jax.numpy as jnp

def _softmax(x, axis=-1):
    return jax.nn.softmax(x, axis=axis)

def _gelu(x):
    return jax.nn.gelu(x, approximate=True)

def _silu(x):
    return jax.nn.silu(x)

def _sigmoid(x):
    return jax.nn.sigmoid(x)

def _layernorm(x, axis=-1, eps=1e-05):
    m = jnp.mean(x, axis=axis, keepdims=True)
    v = jnp.var(x, axis=axis, keepdims=True)
    return (x - m) / jnp.sqrt(v + eps)

def _scatter_add(tgt, idx, src, axis=0):
    return tgt.at[idx].add(src)

def _segment_sum(src, seg, n):
    return jax.ops.segment_sum(src, seg, n)
kernel_name = 'mk_gnn_resnorm_d4_gnn_r8_4e34e4'

def setup_inputs(seed: int=0):
    np.random.seed(seed)
    _w = jnp.asarray

    def _rec_inputs():
        import jax
        import jax.numpy as jnp
        _gk = jax.random.key(seed)
        x = -0.000202 + 1 * jax.random.normal(jax.random.fold_in(_gk, 1), (6250, 128), jnp.float32)
        _s = jax.random.randint(jax.random.fold_in(_gk, 2), (50000,), 0, 6250, jnp.int32)
        _d = jax.random.randint(jax.random.fold_in(_gk, 3), (50000,), 0, 6250, jnp.int32)
        _loop = jnp.arange(6250, dtype=jnp.int32)
        src = jnp.concatenate([_s, _d, _loop])
        dst = jnp.concatenate([_d, _s, _loop])
        _o = jnp.argsort(dst, stable=True)
        src = src[_o]
        dst = dst[_o]
        edge_type_2 = jax.random.randint(jax.random.fold_in(_gk, 13), (106250,), 0, 2, jnp.int32)
        edge_weight = jax.random.uniform(jax.random.fold_in(_gk, 14), (106250,), jnp.float32, 0.0, 1)
        return (x, src, dst, edge_type_2, edge_weight)
    x, src, dst, edge_type_2, edge_weight = _rec_inputs()

    def _L0_gnn_setup():
        import jax, jax.numpy as jnp
        import numpy as np
        N_NODES = 6250
        N_EDGES = 80000
        HIDDEN = 128
        LN_EPS = 1e-05
        key = jax.random.key(seed)
        k_h, k_e, k_w1, k_w2 = jax.random.split(key, 4)
        s = 1.0 / np.sqrt(HIDDEN)
        return {'h': jax.random.normal(k_h, (N_NODES, HIDDEN), dtype=jnp.float32), 'edge_index': jax.random.randint(k_e, (2, N_EDGES), 0, N_NODES, dtype=jnp.int32), 'W1': jax.random.normal(k_w1, (HIDDEN, HIDDEN), dtype=jnp.float32) * s, 'b1': jnp.zeros((HIDDEN,), dtype=jnp.float32), 'W2': jax.random.normal(k_w2, (HIDDEN, HIDDEN), dtype=jnp.float32) * s, 'b2': jnp.zeros((HIDDEN,), dtype=jnp.float32), 'eps': jnp.zeros((), dtype=jnp.float32), 'gamma': jnp.ones((HIDDEN,), dtype=jnp.float32), 'beta': jnp.zeros((HIDDEN,), dtype=jnp.float32)}
    _L0_gnn_all = _L0_gnn_setup()
    _L0_gnn_in = {k: v for k, v in _L0_gnn_all.items() if k in ('W1', 'b1', 'W2', 'b2', 'eps', 'gamma', 'beta')}
    del _L0_gnn_all

    def _L1_gnn_setup():
        import jax, jax.numpy as jnp
        import numpy as np
        N_NODES = 12500
        N_EDGES = 200000
        D_IN, D_HID, D_OUT = (128, 256, 128)

        def _l2norm(v, eps=1e-12):
            n = jnp.linalg.norm(v, axis=-1, keepdims=True)
            return v / jnp.maximum(n, eps)

        def _priv_conv(h, src, dst, n, Wl, bl, Wr, scale):
            xn = _l2norm(h)
            agg = jax.ops.segment_sum(xn[src], dst, num_segments=n)
            h_norm = jnp.linalg.norm(h, axis=-1, keepdims=True)
            out = _l2norm(agg) * h_norm * scale
            out = out @ Wl + bl + h @ Wr
            return _l2norm(out)
        key = jax.random.key(seed)
        ks = jax.random.split(key, 8)
        x = jax.random.normal(ks[0], (N_NODES, D_IN), dtype=jnp.float32)
        edge_index = jax.random.randint(ks[1], (2, N_EDGES), 0, N_NODES, dtype=jnp.int32)
        Wl0 = jax.random.normal(ks[2], (D_IN, D_HID), dtype=jnp.float32) * 0.05
        bl0 = jnp.zeros((D_HID,), dtype=jnp.float32)
        Wr0 = jax.random.normal(ks[3], (D_IN, D_HID), dtype=jnp.float32) * 0.05
        Wl1 = jax.random.normal(ks[4], (D_HID, D_OUT), dtype=jnp.float32) * 0.05
        bl1 = jnp.zeros((D_OUT,), dtype=jnp.float32)
        Wr1 = jax.random.normal(ks[5], (D_HID, D_OUT), dtype=jnp.float32) * 0.05
        scale0 = jnp.ones((), dtype=jnp.float32)
        scale1 = jnp.ones((), dtype=jnp.float32)
        return {'x': x, 'edge_index': edge_index, 'Wl0': Wl0, 'bl0': bl0, 'Wr0': Wr0, 'Wl1': Wl1, 'bl1': bl1, 'Wr1': Wr1, 'scale0': scale0, 'scale1': scale1}
    _L1_gnn_all = _L1_gnn_setup()
    _L1_gnn_in = {k: v for k, v in _L1_gnn_all.items() if k in ('Wl0', 'bl0', 'Wr0', 'Wl1', 'bl1', 'Wr1', 'scale0', 'scale1')}
    del _L1_gnn_all

    def _L2_gnn_setup():
        import jax, jax.numpy as jnp
        import numpy as np
        N_NODES = 6250
        N_EDGES = 100000
        HID = 128
        key = jax.random.key(seed)
        ks = jax.random.split(key, 10)
        s_msg = 1.0 / np.sqrt(2 * HID + 1)
        s_u1 = 1.0 / np.sqrt(2 * HID)
        s_u2 = 1.0 / np.sqrt(HID)
        return {'z': jax.random.normal(ks[0], (N_NODES, HID), dtype=jnp.float32), 'edge_weight': jax.random.uniform(ks[1], (N_EDGES,), dtype=jnp.float32), 'edge_src': jax.random.randint(ks[2], (N_EDGES,), 0, N_NODES), 'edge_dst': jax.random.randint(ks[3], (N_EDGES,), 0, N_NODES), 'Wm': jax.random.normal(ks[4], (2 * HID + 1, HID), dtype=jnp.float32) * s_msg, 'bm': jax.random.normal(ks[5], (HID,), dtype=jnp.float32) * s_msg, 'W1': jax.random.normal(ks[6], (2 * HID, HID), dtype=jnp.float32) * s_u1, 'b1': jax.random.normal(ks[7], (HID,), dtype=jnp.float32) * s_u1, 'W2': jax.random.normal(ks[8], (HID, HID), dtype=jnp.float32) * s_u2, 'b2': jax.random.normal(ks[9], (HID,), dtype=jnp.float32) * s_u2}
    _L2_gnn_all = _L2_gnn_setup()
    _L2_gnn_in = {k: v for k, v in _L2_gnn_all.items() if k in ('Wm', 'bm', 'W1', 'b1', 'W2', 'b2')}
    del _L2_gnn_all

    def _L3_gnn_setup():
        import jax, jax.numpy as jnp
        import numpy as np
        IN_DIM = 128
        OUT_DIM = 128
        N_NODES = 1250
        N_EDGES = 80000
        key = jax.random.key(seed)
        ks = jax.random.split(key, 9)
        X = jax.random.normal(ks[0], (N_NODES, IN_DIM), dtype=jnp.float32)
        edge_index = jax.random.randint(ks[1], (2, N_EDGES), 0, N_NODES, dtype=jnp.int64)
        edge_types = jax.random.randint(ks[2], (N_EDGES,), 0, 2, dtype=jnp.int64)
        s = 1.0 / np.sqrt(IN_DIM)
        W_data = jax.random.uniform(ks[3], (OUT_DIM, IN_DIM), minval=-s, maxval=s, dtype=jnp.float32)
        b_data = jax.random.uniform(ks[4], (OUT_DIM,), minval=-s, maxval=s, dtype=jnp.float32)
        W_control = jax.random.uniform(ks[5], (OUT_DIM, IN_DIM), minval=-s, maxval=s, dtype=jnp.float32)
        b_control = jax.random.uniform(ks[6], (OUT_DIM,), minval=-s, maxval=s, dtype=jnp.float32)
        W_self = jax.random.uniform(ks[7], (OUT_DIM, IN_DIM), minval=-s, maxval=s, dtype=jnp.float32)
        b_self = jax.random.uniform(ks[8], (OUT_DIM,), minval=-s, maxval=s, dtype=jnp.float32)
        return {'X': X, 'edge_index': edge_index, 'edge_types': edge_types, 'W_data': W_data, 'b_data': b_data, 'W_control': W_control, 'b_control': b_control, 'W_self': W_self, 'b_self': b_self}
    _L3_gnn_all = _L3_gnn_setup()
    _L3_gnn_in = {k: v for k, v in _L3_gnn_all.items() if k in ('W_data', 'b_data', 'W_control', 'b_control', 'W_self', 'b_self')}
    del _L3_gnn_all
    return {'x': x, 'src': src, 'dst': dst, 'edge_type_2': edge_type_2, 'edge_weight': edge_weight, 'L0_gnn_W1': _L0_gnn_in['W1'], 'L0_gnn_b1': _L0_gnn_in['b1'], 'L0_gnn_W2': _L0_gnn_in['W2'], 'L0_gnn_b2': _L0_gnn_in['b2'], 'L0_gnn_eps': _L0_gnn_in['eps'], 'L0_gnn_gamma': _L0_gnn_in['gamma'], 'L0_gnn_beta': _L0_gnn_in['beta'], 'L1_gnn_Wl0': _L1_gnn_in['Wl0'], 'L1_gnn_bl0': _L1_gnn_in['bl0'], 'L1_gnn_Wr0': _L1_gnn_in['Wr0'], 'L1_gnn_Wl1': _L1_gnn_in['Wl1'], 'L1_gnn_bl1': _L1_gnn_in['bl1'], 'L1_gnn_Wr1': _L1_gnn_in['Wr1'], 'L1_gnn_scale0': _L1_gnn_in['scale0'], 'L1_gnn_scale1': _L1_gnn_in['scale1'], 'L2_gnn_Wm': _L2_gnn_in['Wm'], 'L2_gnn_bm': _L2_gnn_in['bm'], 'L2_gnn_W1': _L2_gnn_in['W1'], 'L2_gnn_b1': _L2_gnn_in['b1'], 'L2_gnn_W2': _L2_gnn_in['W2'], 'L2_gnn_b2': _L2_gnn_in['b2'], 'L3_gnn_W_data': _L3_gnn_in['W_data'], 'L3_gnn_b_data': _L3_gnn_in['b_data'], 'L3_gnn_W_control': _L3_gnn_in['W_control'], 'L3_gnn_b_control': _L3_gnn_in['b_control'], 'L3_gnn_W_self': _L3_gnn_in['W_self'], 'L3_gnn_b_self': _L3_gnn_in['b_self']}

def reference(x, src, dst, edge_type_2, edge_weight, L0_gnn_W1, L0_gnn_b1, L0_gnn_W2, L0_gnn_b2, L0_gnn_eps, L0_gnn_gamma, L0_gnn_beta, L1_gnn_Wl0, L1_gnn_bl0, L1_gnn_Wr0, L1_gnn_Wl1, L1_gnn_bl1, L1_gnn_Wr1, L1_gnn_scale0, L1_gnn_scale1, L2_gnn_Wm, L2_gnn_bm, L2_gnn_W1, L2_gnn_b1, L2_gnn_W2, L2_gnn_b2, L3_gnn_W_data, L3_gnn_b_data, L3_gnn_W_control, L3_gnn_b_control, L3_gnn_W_self, L3_gnn_b_self):
    import jax
    import jax.numpy as jnp

    def _L0_gnn_ref(h, edge_index, W1, b1, W2, b2, eps, gamma, beta):
        import jax, jax.numpy as jnp
        import numpy as np
        N_NODES = 6250
        N_EDGES = 80000
        HIDDEN = 128
        LN_EPS = 1e-05
        src, dst = (edge_index[0], edge_index[1])
        agg = jax.ops.segment_sum(h[src], dst, num_segments=h.shape[0])
        z = (1.0 + eps) * h + agg
        z = jax.nn.relu(z @ W1.T + b1)
        h_conv = z @ W2.T + b2
        h_res = h_conv + h
        mu = jnp.mean(h_res, axis=-1, keepdims=True)
        var = jnp.var(h_res, axis=-1, keepdims=True)
        h_norm = (h_res - mu) * jax.lax.rsqrt(var + LN_EPS) * gamma + beta
        return jax.nn.relu(h_norm)

    def _L1_gnn_ref(x, edge_index, Wl0, bl0, Wr0, Wl1, bl1, Wr1, scale0, scale1):
        import jax, jax.numpy as jnp
        import numpy as np
        N_NODES = 12500
        N_EDGES = 200000
        D_IN, D_HID, D_OUT = (128, 256, 128)

        def _l2norm(v, eps=1e-12):
            n = jnp.linalg.norm(v, axis=-1, keepdims=True)
            return v / jnp.maximum(n, eps)

        def _priv_conv(h, src, dst, n, Wl, bl, Wr, scale):
            xn = _l2norm(h)
            agg = jax.ops.segment_sum(xn[src], dst, num_segments=n)
            h_norm = jnp.linalg.norm(h, axis=-1, keepdims=True)
            out = _l2norm(agg) * h_norm * scale
            out = out @ Wl + bl + h @ Wr
            return _l2norm(out)
        n = x.shape[0]
        loops = jnp.arange(n, dtype=edge_index.dtype)
        src = jnp.concatenate([edge_index[0], loops])
        dst = jnp.concatenate([edge_index[1], loops])
        h = _priv_conv(x, src, dst, n, Wl0, bl0, Wr0, scale0)
        h = jax.nn.relu(h)
        h = _priv_conv(h, src, dst, n, Wl1, bl1, Wr1, scale1)
        return h

    def _L2_gnn_ref(z, edge_weight, edge_src, edge_dst, Wm, bm, W1, b1, W2, b2):
        import jax, jax.numpy as jnp
        import numpy as np
        N_NODES = 6250
        N_EDGES = 100000
        HID = 128
        n, H = z.shape
        Wd, Ws, ww = (Wm[:H], Wm[H:2 * H], Wm[2 * H])
        msgs = z[edge_dst] @ Wd + z[edge_src] @ Ws + edge_weight[:, None] * ww[None, :] + bm
        agg = jax.ops.segment_max(msgs, edge_dst, num_segments=n)
        deg = jax.ops.segment_sum(jnp.ones_like(edge_weight), edge_dst, num_segments=n)
        agg = jnp.where(deg[:, None] > 0, agg, jnp.zeros((), dtype=z.dtype))
        W1a, W1b = (W1[:H], W1[H:])
        hidden = jax.nn.relu(z @ W1a + agg @ W1b + b1)
        return hidden @ W2 + b2

    def _L3_gnn_ref(X, edge_index, edge_types, W_data, b_data, W_control, b_control, W_self, b_self):
        import jax, jax.numpy as jnp
        import numpy as np
        IN_DIM = 128
        OUT_DIM = 128
        N_NODES = 1250
        N_EDGES = 80000
        src, dst = (edge_index[0], edge_index[1])
        Xs = X[src]
        m_data = Xs @ W_data.T + b_data
        m_ctrl = Xs @ W_control.T + b_control
        msg = jnp.where((edge_types == 0)[:, None], m_data, m_ctrl)
        agg = jax.ops.segment_sum(msg, dst, num_segments=X.shape[0])
        out = agg + (X @ W_self.T + b_self)
        return jax.nn.relu(out)
    edge_index = jnp.stack([src, dst])
    x = _layernorm(x + _L0_gnn_ref(x, edge_index, L0_gnn_W1, L0_gnn_b1, L0_gnn_W2, L0_gnn_b2, L0_gnn_eps, L0_gnn_gamma, L0_gnn_beta), axis=-1)
    x = _layernorm(x + _L1_gnn_ref(x, edge_index, L1_gnn_Wl0, L1_gnn_bl0, L1_gnn_Wr0, L1_gnn_Wl1, L1_gnn_bl1, L1_gnn_Wr1, L1_gnn_scale0, L1_gnn_scale1), axis=-1)
    x = _layernorm(x + _L2_gnn_ref(x, edge_weight, src, dst, L2_gnn_Wm, L2_gnn_bm, L2_gnn_W1, L2_gnn_b1, L2_gnn_W2, L2_gnn_b2), axis=-1)
    x = _layernorm(x + _L3_gnn_ref(x, edge_index, edge_type_2, L3_gnn_W_data, L3_gnn_b_data, L3_gnn_W_control, L3_gnn_b_control, L3_gnn_W_self, L3_gnn_b_self), axis=-1)
    return x

_drawn_inputs = setup_inputs


def setup_inputs(seed=0):
    import zlib

    import numpy as np

    out = dict(_drawn_inputs(seed))
    spreads = {'L0_gnn_b1': (0.0, 0.696),
     'L0_gnn_b2': (0.0, 0.363),
     'L0_gnn_gamma': (1.0, 0.2),
     'L0_gnn_beta': (0.0, 0.1),
     'L1_gnn_bl0': (0.0, 2.0),
     'L1_gnn_bl1': (0.0, 0.1)}
    factors = {'edge_weight': 8.0, 'L1_gnn_Wr0': 24.597, 'L3_gnn_b_self': 3.918, 'L1_gnn_Wl0': 12.572}
    for name, (base, spread) in spreads.items():
        noise = np.random.default_rng([zlib.crc32(name.encode()), seed]).standard_normal(out[name].shape)
        drawn = base * np.exp(spread * noise) if base else spread * noise
        out[name] = jnp.asarray(drawn.astype(out[name].dtype))
    for name, factor in factors.items():
        out[name] = (out[name] * factor).astype(out[name].dtype)
    return out
```

```python
from contextlib import ExitStack

import numpy as np

import concourse.bass as bass
from concourse import mybir

F32 = mybir.dt.float32
BF16 = mybir.dt.bfloat16
I32 = mybir.dt.int32
AX_X = mybir.AxisListType.X
ALU = mybir.AluOpType
ACT = mybir.ActivationFunctionType

P = 128
H = 128
H2 = 256
N = 6250
E = 106250
NT = -(-N // P)
NP = NT * P
N_ET = -(-E // P)
STEPS = N_ET + NT - 1
SC = -(-STEPS // P)
ROWS = SC * P
LAG = NT - 1
RING = 64
SLOT = 264
UP = 136
AHEAD = RING - LAG
GROUPS = (8, 8, 8, 8, 8, 5, 4)
START = [sum(GROUPS[:g]) for g in range(len(GROUPS) + 1)]
NG = len(GROUPS)
GMAX = max(GROUPS)
OH_BATCH = 4
OH_RING = 3 * OH_BATCH
REGS = 8
NO_NODE = 8192
BIG = 3.3895313892515355e38
LN_EPS = 1e-5
NORM_EPS2 = 1e-24
assert START[-1] == NT and AHEAD > 0 and ROWS >= N_ET
MARGIN = 10
DONE_BY = [min(STEPS, -(-START[g + 1] * STEPS // NT) + MARGIN) for g in range(NG - 1)] + [STEPS]
NEWEST = [min(s, N_ET - 1, s * N_ET // STEPS + MARGIN) for s in range(STEPS)]


class Engine:

    def __init__(self, sem, eng, name):
        self.new_sem, self.eng, self.name = sem, eng, name
        self.waited = {}
        self.last = None

    def stage(self, stage):
        self.key = f"{self.name}_{stage}"
        self.sem, self.count = self.new_sem(self.key), 0

    def do(self, instruction):
        self.count += 1
        instruction.then_inc(self.sem, 1)
        self.last = (self.key, self.sem, self.count)
        return self.last

    def after(self, *points):
        for point in points:
            if point is None:
                continue
            key, sem, value = point
            if self.waited.get(key, 0) < value:
                self.waited[key] = value
                self.eng.wait_ge(sem, value)


class Loads:

    def __init__(self, sem, name):
        self.key, self.sem, self.count = name, sem(name), 0

    def add(self, instruction):
        self.count += 16
        instruction.then_inc(self.sem, 16)
        return (self.key, self.sem, self.count)

    @property
    def point(self):
        return (self.key, self.sem, self.count)


def build(nc, a, out):
    ctx = ExitStack()
    with ctx:
        def sb(name, shape, dt=F32):
            return ctx.enter_context(nc.sbuf_tensor(name, shape, dt))

        def dram(name, shape, dt=F32):
            return nc.dram_tensor(name, shape, dt, kind="Internal").ap()

        semaphores = {}

        def sem(name):
            if name not in semaphores:
                semaphores[name] = ctx.enter_context(nc.semaphore(name))
            return semaphores[name]

        pe, ve, ac, po, sp = engines = [Engine(sem, e, n) for e, n in (
            (nc.tensor, "pe"), (nc.vector, "ve"), (nc.scalar, "ac"), (nc.gpsimd, "po"), (nc.sync, "sp"))]
        V, A, T, G, S = nc.vector, nc.scalar, nc.tensor, nc.gpsimd, nc.sync
        for e in (pe, ve, ac):
            e.stage("prep")

        X = sb("x_nodes", [P, NT, H])
        ACC = sb("acc", [P, NT * SLOT])
        RG = sb("ring", [P, RING * SLOT])
        OH = sb("onehot", [P, OH_RING, P])
        LOC = sb("loc", [P, ROWS])
        LOCEND = sb("loc_end", [P, ROWS])
        SRC = sb("src_cols", [P, N_ET], I32)
        BASES = sb("bases", [2, ROWS], I32)
        CST = sb("consts", [P, 3 * P + SC + 1 + SC + NT])
        ZT = sb("zt", [P, GMAX * H2])
        HT = sb("ht", [P, GMAX * H2])
        JUNK = sb("junk", [P, 4, H2])
        MASK = sb("mask", [P, 2, 512], BF16)
        WEIGHT = sb("edge_weights", [P, N_ET])
        FLAG = sb("irregular", [1, 1], I32)
        one_eps = sb("one_plus_eps", [P, 1])
        ST = sb("bn_parts", [P, GMAX, 6])
        MV = sb("mean_var", [P, NT, 2])
        RSTD = sb("rstd", [P, NT])
        NMR = sb("neg_mean_rstd", [P, NT])
        SS = sb("sumsq", [P, 3, NT])
        NRM = sb("norms", [P, 3, NT])
        RN = sb("rnorms", [P, 3, NT])
        HN = sb("h_norm", [P, 2, NT])
        IDENT, SHIFT2 = CST[:, 0:P], CST[:, 0:2 * P]
        IOTA = CST[:, 2 * P:3 * P]
        STEPNO, BOUND = CST[:, 3 * P:3 * P + SC], CST[:, 3 * P + SC:3 * P + SC + 1]
        AT_MOST = CST[:, 3 * P + SC + 1:3 * P + 2 * SC + 1]
        END_BY = CST[:, 3 * P + 2 * SC + 1:]
        ACC3 = ACC[:, :].rearrange("p (t c) -> p t c", c=SLOT)
        AUX3 = ACC3[:, :, UP:UP + H]
        RG3 = RG[:, :].rearrange("p (t c) -> p t c", c=SLOT)
        bank = [ctx.enter_context(nc.psum_tensor(f"bank{b}", [P, 512], F32)) for b in range(8)]

        wload = Loads(sem, "load_weights")

        def weight(name, src, shape):
            w = sb(name, shape)
            wload.add(S.dma_start(w[:], src))
            return w

        def row(name, *srcs):
            n = sum(s.shape[-1] for s in srcs)
            w, at = sb(name, [P, n]), 0
            for s in srcs:
                k = s.shape[-1]
                wload.add(S.dma_start(w[:, at:at + k], s.to_broadcast([P, k])))
                at += k
            return w

        xload = Loads(sem, "load_x")
        iload = Loads(sem, "load_indices")
        iload.add(S.dma_start(SRC[:], a["src_cols"]))
        DROWS = ZT[:, 0:ROWS].bitcast(I32).rearrange("p (c e) -> p c e", e=P)
        dload = Loads(sem, "load_dst")
        dload.add(S.dma_start(CST[:], a["consts"]))
        dload.add(S.dma_start(DROWS, a["dst_rows"].rearrange("(c p) e -> p c e", p=P)))
        TYPE = HT[:, 0:N_ET].bitcast(I32)
        DPREV = ZT[:, ROWS:2 * ROWS].bitcast(I32)
        tload = Loads(sem, "load_type_prev")
        tload.add(S.dma_start(TYPE, a["type_cols"]))
        tload.add(S.dma_start(DPREV.rearrange("p (c e) -> p c e", e=P),
                              a["prev_rows"].rearrange("(c p) e -> p c e", p=P)))
        for g in range(NG):
            tiles = slice(START[g], START[g + 1])
            xload.add(S.dma_start(X[:, tiles, :], a["x"].rearrange("(t p) h -> p t h", p=P)[:, tiles, :]))
        w1t0 = weight("l0_w1t", a["l0_w1t"], [P, H])
        w2t0 = weight("l0_w2t", a["l0_w2t"], [P, H])
        b1_0 = weight("l0_b1", a["l0_b1"].rearrange("o p -> p o"), [P, 1])
        b2_0, gam, bet = row("l0_b2", a["l0_b2"]), row("l0_gamma", a["l0_gamma"]), row("l0_beta", a["l0_beta"])
        scal = row("scalars", a["l0_eps"], a["l1_scale0"], a["l1_scale1"])
        wl0 = weight("l1_wl0", a["l1_wl0"], [P, H2])
        wr0 = weight("l1_wr0", a["l1_wr0"], [P, H2])
        bl0, bl1 = row("l1_bl0", a["l1_bl0"]), row("l1_bl1", a["l1_bl1"])
        wl1 = weight("l1_wl1", a["l1_wl1"].rearrange("(k p) h -> p k h", p=P), [P, 2, H])
        wr1 = weight("l1_wr1", a["l1_wr1"].rearrange("(k p) h -> p k h", p=P), [P, 2, H])
        wms = weight("l2_wm", a["l2_wm"][0:2 * H, :].rearrange("(k p) h -> p k h", p=P), [P, 2, H])
        ww = row("l2_ww", a["l2_wm"][2 * H:2 * H + 1, :])
        wload.add(S.dma_start(WEIGHT[:], a["weight_cols"]))
        bm = row("l2_bm", a["l2_bm"])
        w1_2 = weight("l2_w1", a["l2_w1"].rearrange("(k p) h -> p k h", p=P), [P, 2, H])
        b1_2 = weight("l2_b1", a["l2_b1"].rearrange("o p -> p o"), [P, 1])
        w2_2 = weight("l2_w2", a["l2_w2"], [P, H])
        b2_2 = row("l2_b2", a["l2_b2"])
        wdc = sb("l3_wdc", [P, 2, H])
        wload.add(S.dma_start(wdc[:, 0, :], a["l3_wdt"]))
        wload.add(S.dma_start(wdc[:, 1, :], a["l3_wct"]))
        bdc = row("l3_bdc", a["l3_bd"], a["l3_bc"])
        wst = weight("l3_wst", a["l3_wst"], [P, H])
        bs = row("l3_bs", a["l3_bs"])
        eps_col = sb("ln_eps", [P, 1])
        eps_ready = ve.do(V.memset(eps_col[:], LN_EPS))

        tab = {"l0": a["x"], "l1a": dram("tab_l1a", [NP, H]), "l1b": dram("tab_l1b", [NP, H2]),
               "l2": dram("tab_l2", [NP, H]), "l3": dram("tab_l3", [2 * NP, H])}
        mask_dram = dram("scan_mask", [1, ROWS * P], BF16)
        src3_dram = dram("src_type_cols", [P, N_ET], I32)
        aux1_dram = dram("h1_wr1", [NP, H])

        gathered = [Loads(sem, f"gathered{k}") for k in range(AHEAD)]

        def gather(i, table, width, at=0):
            return gathered[i % AHEAD].add(G.indirect_dma_start(
                RG3[:, i % RING, at:at + width], None, table, bass.IndirectOffsetOnAxis(ap=SRC[:, i:i + 1], axis=0)))

        first = {}

        def first_gathers(upto):
            for i in range(len(first), upto):
                po.after(first.get(i - AHEAD))
                first[i] = gather(i, tab["l0"], H)

        po.after(iload.point)
        first_gathers(10)

        W = ACC[:, :]
        col = lambda at, n=1: W[:, at:at + n]
        FIRST, CMP, TK, CNT = col(0, SC), col(16, SC * P), col(8), col(9)
        BK, BKI, FL, CE = col(10), col(11).bitcast(I32), col(12), col(13)
        TKI = col(14).bitcast(I32)
        ve.after(dload.point)
        t = ve.do(V.tensor_copy(FIRST, DROWS[:, :, 0]))
        ve.after(t)
        KROW = col(2000, P)
        t = ve.do(V.tensor_scalar(KROW, IOTA, 1.0, float(P), ALU.add, ALU.mult))
        ve.after(t)
        for c in range(SC):
            t = ve.do(V.tensor_scalar(CMP[:, c * P:(c + 1) * P], KROW, FIRST[:, c:c + 1], None, ALU.is_gt))
        ones = sb("ones", [P, 1])
        t = ve.do(V.memset(ones[:], 1.0))
        pe.after(t, dload.point)
        for c in range(SC):
            t = pe.do(T.matmul(bank[0][:, 0:1], CMP[:, c * P:(c + 1) * P], ones[:], start=c == 0, stop=c == SC - 1))
        ve.after(t)
        t = ve.do(V.tensor_scalar(TK, bank[0][:, 0:1], -1.0, 0.0, ALU.add, ALU.max))
        ve.after(t)
        t = ve.do(V.tensor_copy(TKI, TK))
        po.after(t)
        rows_of = Loads(sem, "gather_boundary_rows")
        BROWS = col(2200, P).bitcast(I32)
        rows_of.add(G.indirect_dma_start(BROWS, None, a["dst_rows"], bass.IndirectOffsetOnAxis(ap=TKI, axis=0)))
        first_gathers(32)
        ve.after(rows_of.point)
        BROWF = col(2400, P)
        t = ve.do(V.tensor_copy(BROWF, BROWS))
        ve.after(t)
        t = ve.do(V.tensor_scalar(col(2600, P), BROWF, BOUND, None, ALU.is_lt, ALU.add, accum_out=CNT))
        ve.after(t)
        t = ve.do(V.scalar_tensor_tensor(BK, TK, float(P), CNT, ALU.mult, ALU.add))
        ve.after(t)
        t = ve.do(V.tensor_copy(BKI, BK))
        ve.after(t)
        FLI, CEI, BPI = col(15).bitcast(I32), col(2800).bitcast(I32), col(2801).bitcast(I32)
        BP = col(2802)
        ve.do(V.tensor_scalar(FLI, BKI, 7, None, ALU.logical_shift_right))
        t = ve.do(V.tensor_scalar(BP, BK, float(P - 1), None, ALU.add))
        ve.after(t)
        t = ve.do(V.tensor_copy(BPI, BP))
        ve.after(t)
        t = ve.do(V.tensor_scalar(CEI, BPI, 7, None, ALU.logical_shift_right))
        ve.after(t)
        ve.do(V.tensor_copy(FL, FLI))
        t = ve.do(V.tensor_copy(CE, CEI))
        pe.after(t)
        for b, v in ((1, BK), (2, FL), (3, CE)):
            t = pe.do(T.matmul(bank[b][:, 0:2 * P], v.to_broadcast([P, P]), SHIFT2, start=True, stop=True))
        ve.after(t)
        ROWB, ROWF, ROWC = col(3000, 2 * P), col(3300, 2 * P), col(3600, 2 * P)
        for b, v in ((1, ROWB), (2, ROWF), (3, ROWC)):
            t = ve.do(V.tensor_copy(v, bank[b][:, 0:2 * P]))
        ve.after(t)
        NOTEMPTY, NSTEP, TEND, DIFF = col(3900, NT), col(3960, NT), col(4020, NT), col(4080, NT)
        ONEROW = col(4140, NT)
        ve.do(V.tensor_tensor(NOTEMPTY, ROWB[:, 0:NT], ROWB[:, P:P + NT], ALU.is_gt))
        ve.do(V.tensor_tensor(NSTEP, ROWC[:, 0:NT], ROWF[:, P:P + NT], ALU.subtract))
        ve.do(V.memset(ONEROW, 1.0))
        t = ve.do(V.tensor_tensor(DIFF, ROWF[:, 0:NT], ROWF[:, P:P + NT], ALU.subtract))
        ve.after(t)
        t = ve.do(V.tensor_tensor(NSTEP, NSTEP, NOTEMPTY, ALU.mult))
        ve.after(t)
        ve.do(V.tensor_tensor_scan(TEND, ONEROW, NSTEP, 0.0, ALU.mult, ALU.add))
        t = ve.do(V.tensor_tensor(DIFF, DIFF, NSTEP, ALU.subtract))
        ve.after(t)
        JS, IS, JC, SUB = col(4200, SC), col(4210, SC), col(4220, SC), col(4230, SC)
        ISUM = col(4240, SC)
        for c in range(SC):
            GE = col(4300 + 64 * c, NT)
            t = ve.do(V.tensor_scalar(GE, TEND, STEPNO[:, c:c + 1], None, ALU.is_le, ALU.add, accum_out=JS[:, c:c + 1]))
            ve.after(t)
            t = ve.do(V.tensor_tensor_reduce(out=col(4800 + 64 * c, NT), in0=GE, in1=DIFF, scale=1.0, scalar=0.0,
                                             op0=ALU.mult, op1=ALU.add, accum_out=ISUM[:, c:c + 1]))
        ve.after(t)
        t = ve.do(V.tensor_tensor(IS, ISUM, STEPNO, ALU.add))
        ve.after(t)
        ISF, ISI = col(5300, SC), col(5310, SC).bitcast(I32)
        ve.do(V.tensor_scalar(ISF, IS, float(N_ET - 1), None, ALU.min))
        ve.do(V.tensor_scalar(JC, JS, float(NT - 1), float(SLOT), ALU.min, ALU.mult))
        t = ve.do(V.tensor_scalar(SUB, JS, float(P), None, ALU.mult))
        ve.after(t)
        is_ready = ve.do(V.tensor_copy(ISI, ISF))
        po.after(is_ready)
        DCUR, DNXT = col(5400, ROWS).bitcast(I32), col(6300, ROWS).bitcast(I32)
        step_rows = Loads(sem, "gather_step_rows")
        for c in range(SC):
            for rows, src in ((DCUR, a["dst_rows"]), (DNXT, a["next_rows"])):
                step_rows.add(G.indirect_dma_start(rows[:, c * P:(c + 1) * P], None, src,
                                                   bass.IndirectOffsetOnAxis(ap=ISI[:, c:c + 1], axis=0)))
        first_gathers(RING - 4)
        EARLY, LATE, BAD = col(12840, SC), col(12850, NT), col(12900, 2)
        ve.after(is_ready)
        ve.do(V.tensor_tensor(EARLY, ISF, AT_MOST, ALU.is_gt))
        t = ve.do(V.tensor_tensor(LATE, TEND, END_BY, ALU.is_gt))
        ve.after(t)
        ve.do(V.tensor_reduce(BAD[:, 0:1], EARLY, AX_X, ALU.add))
        t = ve.do(V.tensor_reduce(BAD[:, 1:2], LATE, AX_X, ALU.add))
        ve.after(t)
        BADSUM = col(12910)
        t = ve.do(V.tensor_tensor(BADSUM, BAD[:, 0:1], BAD[:, 1:2], ALU.add))
        pe.after(t)
        t = pe.do(T.matmul(bank[5][0:1, 0:1], BADSUM, ones[:], start=True, stop=True))
        ve.after(t)
        flag_ready = ve.do(V.tensor_copy(FLAG[:], bank[5][0:1, 0:1]))
        ve.after(is_ready)
        SLI, SLF = col(5320, SC).bitcast(I32), col(5330, 2 * SC)
        t = ve.do(V.tensor_scalar(SLI, ISI, RING - 1, None, ALU.bitwise_and))
        ve.after(t)
        ve.do(V.tensor_scalar(SLF[:, 0:SC], SLI, float(SLOT), None, ALU.mult))
        t = ve.do(V.tensor_copy(SLF[:, SC:2 * SC], JC))
        pe.after(t)
        pe.do(T.transpose(bank[4][0:SC, 0:P], SLF[:, 0:SC], IDENT))
        t = pe.do(T.transpose(bank[4][0:SC, P:2 * P], SLF[:, SC:2 * SC], IDENT))
        ve.after(t)
        BROW2 = W[0:SC, 7200:7200 + 2 * P].bitcast(I32)
        t = ve.do(V.tensor_copy(BROW2, bank[4][0:SC, 0:2 * P]))
        sp.after(t)
        bases = Loads(sem, "move_bases")
        for n in range(2):
            bases.add(S.dma_start(BASES[n:n + 1, :], BROW2[:, n * P:(n + 1) * P]))
        ve.after(tload.point, iload.point)
        SRC3 = col(12000, N_ET).bitcast(I32)
        t = ve.do(V.scalar_tensor_tensor(SRC3, SRC[:], 2.0, TYPE, ALU.mult, ALU.add))
        sp.after(t)
        src3_stored = Loads(sem, "store_src3")
        src3_stored.add(S.dma_start(src3_dram, SRC3))
        NEQ = col(7500, ROWS)
        t = ve.do(V.tensor_tensor(NEQ, ZT[:, 0:ROWS].bitcast(I32), DPREV, ALU.not_equal))
        ve.after(t)
        t = ve.do(V.tensor_scalar(NEQ, NEQ, -2.0, 1.0, ALU.mult, ALU.add))
        ve.after(t)
        MASKV = col(8400, ROWS // 2).bitcast(BF16)
        t = ve.do(V.tensor_scalar(MASKV, NEQ, BIG, None, ALU.mult))
        sp.after(t)
        mask_stored = Loads(sem, "store_mask")
        mask_stored.add(S.dma_start(mask_dram.rearrange("o (c p e) -> (o p) c e", p=P, e=P),
                                    MASKV.rearrange("p (c e) -> p c e", e=P)))
        ve.after(step_rows.point)
        LC, LE = col(8900, ROWS), col(9800, ROWS)
        NE = col(10700, ROWS)
        for c in range(SC):
            ve.do(V.tensor_scalar(LC[:, c * P:(c + 1) * P], DCUR[:, c * P:(c + 1) * P], SUB[:, c:c + 1], None,
                                  ALU.subtract))
        t = ve.do(V.tensor_tensor(NE, DCUR, DNXT, ALU.not_equal))
        ve.after(t)
        t = ve.do(V.scalar_tensor_tensor(LE, LC, 1.0, NE, ALU.add, ALU.mult))
        ve.after(t)
        t = ve.do(V.tensor_scalar(LE, LE, -1.0, None, ALU.add))
        pe.after(t)
        for n, (v, dst) in enumerate(((LC, LOC), (LE, LOCEND))):
            for h in range(2):
                c0, c1 = (0, 4) if h == 0 else (4, SC)
                for c in range(c0, c1):
                    t = pe.do(T.transpose(bank[2 * n + h][:, (c - c0) * P:(c - c0 + 1) * P], v[:, c * P:(c + 1) * P], IDENT))
                ve.after(t)
                tables = ve.do(V.tensor_copy(dst[:, c0 * P:c1 * P], bank[2 * n + h][:, 0:(c1 - c0) * P]))

        regs = {e.name: [e.eng.alloc_register(f"{e.name}_base{q}") for q in range(REGS)] for e in (pe, ve)}

        def base(e, n, s, top):
            r = regs[e.name]
            if s % REGS == 0:
                e.after(bases.point)
                e.eng.load(r, BASES[n:n + 1, s:s + REGS])
            return e.eng.snap(r[s % REGS], min_val=0, max_val=top)

        class Steps:
            ADD_LAG = 2
            PAIR = 2

            def __init__(self, regular, locs, cols, banks, tile_ready, acc_ready):
                self.regular, self.locs, self.cols, self.banks = regular, locs, cols, banks
                self.tile_ready, self.acc_ready = tile_ready, acc_ready
                self.product, self.added, self.hot = {}, {}, {}
                self.work, self.last_work = [], 0

            def place(self, s):
                return bank[self.banks[s // self.PAIR % len(self.banks)]][:, (s % self.PAIR) * H2:(s % self.PAIR) * H2 + self.cols]

            def node_work(self, stages):
                for g in range(NG):
                    room = DONE_BY[g + 1] - DONE_BY[g] if g + 1 < NG else 0
                    pace = max(1, min(4, room // len(stages)))
                    self.work += [(DONE_BY[g] if self.regular else STEPS, pace, stage, g) for stage in stages]

            def add(self, s):
                ve.after(self.product[min(s | 1, STEPS - 1)], self.acc_ready, self.added.get(s - 1))
                dst = ACC[:, bass.ds(base(ve, 1, s, (NT - 1) * SLOT), self.cols)]
                self.added[s] = ve.do(V.tensor_tensor(dst, dst, self.place(s), ALU.add))

            def one_hots(self, s):
                n = min(OH_BATCH, STEPS - s)
                ve.after(self.product.get(s + n - 1 - OH_RING))
                self.hot[s // OH_BATCH] = ve.do(V.tensor_tensor(
                    OH[:, s % OH_RING:s % OH_RING + n, :], IOTA.unsqueeze(1).to_broadcast([P, n, P]),
                    self.locs[:, s:s + n].unsqueeze(2).to_broadcast([P, n, P]), ALU.is_equal))

            def step(self, s):
                if s == 0:
                    self.one_hots(0)
                if s % OH_BATCH == 0 and s + OH_BATCH < STEPS:
                    self.one_hots(s + OH_BATCH)
                if s >= self.ADD_LAG:
                    self.add(s - self.ADD_LAG)
                tile = RG[:, bass.ds(base(pe, 0, s, (RING - 1) * SLOT), self.cols)]
                newest = NEWEST[s] if self.regular else min(s, N_ET - 1)
                pe.after(self.hot[s // OH_BATCH], self.added.get((s | 1) - self.PAIR * len(self.banks)), self.tile_ready[newest])
                self.product[s] = pe.do(T.matmul(self.place(s), OH[:, s % OH_RING, :], tile, start=True, stop=True))
                if self.work:
                    ready, pace, stage, g = self.work[0]
                    if s >= ready + self.ADD_LAG and s >= self.last_work + pace:
                        self.work.pop(0)
                        self.last_work = s
                        stage(g, self.added[DONE_BY[g] - 1])

            def finish(self):
                for s in range(STEPS - self.ADD_LAG, STEPS):
                    self.add(s)
                for _, _, stage, g in self.work:
                    stage(g, self.added[(DONE_BY[g] if self.regular else STEPS) - 1])

        gtiles = lambda g: range(START[g], START[g + 1])
        gslice = lambda g: slice(START[g], START[g + 1])
        wide = lambda ap, c: ap.rearrange("p (t c) -> p t c", c=c)
        spread = lambda bias, n, c: bias[:, 0:c].unsqueeze(1).to_broadcast([P, n, c])
        xt = lambda j: X[:, j, :]
        at = lambda w: lambda j: ACC3[:, j, 0:w]
        aux = lambda j: AUX3[:, j, :]
        NODE_BANKS = (4, 5, 6, 7)
        LOW, HIGH = (4, 5), (6, 7)
        table_rows = lambda t, g, k=1: t.rearrange("(t p k) c -> p t (k c)", p=P, k=k)[:, gslice(g), :]

        def parts(g, per):
            return [(b, q, min(per, GROUPS[g] - q)) for b, q in enumerate(range(0, GROUPS[g], per))]

        def transposes(pt, g, src, width, banks, *before):
            pe.after(*before)
            n = 0
            for j in gtiles(g):
                for b in range(width // P):
                    pt[g] = pe.do(T.transpose(bank[banks[n // 4]][:, (n % 4) * P:(n % 4 + 1) * P],
                                              src(j)[:, b * P:(b + 1) * P], IDENT))
                    n += 1

        def copy_out(pt, g, dst, width, banks, *before):
            ac.after(*before)
            for b, lo in enumerate(range(0, GROUPS[g] * width, 512)):
                m = min(512, GROUPS[g] * width - lo)
                pt[g] = ac.do(A.copy(dst[:, lo:lo + m], bank[banks[b]][:, 0:m]))

        def copy_out_aux(pt, g, banks, *before):
            ac.after(*before)
            for b, q, n in parts(g, 4):
                j = START[g] + q
                pt[g] = ac.do(A.copy(AUX3[:, j:j + n, :], wide(bank[banks[b]][:, 0:n * P], P)))

        def products(pt, g, lhsT, rhs, width, banks, *before):
            pe.after(*before)
            per = 512 // width
            for q in range(GROUPS[g]):
                left = lhsT(q)
                for k in range(len(rhs)):
                    pt[g] = pe.do(T.matmul(bank[banks[q // per]][:, (q % per) * width:(q % per + 1) * width], left[k], rhs[k],
                                           start=k == 0, stop=k == len(rhs) - 1))

        blocks = lambda buf, k=1: lambda q: [buf[:, (k * q + b) * P:(k * q + b + 1) * P] for b in range(k)]

        def layer_norm(src, dst, before, st, sd, iv, nm):
            def stats(g, _):
                ve.after(before[g], iv.get(g - 1))
                for q, j in enumerate(gtiles(g)):
                    t = ve.do(V.bn_stats(ST[:, q, :], src(j)))
                ve.after(t)
                for q, j in enumerate(gtiles(g)):
                    st[g] = ve.do(V.bn_aggr(MV[:, j, :], ST[:, q, :]))

            def deviation(g, _):
                ac.after(st[g], eps_ready)
                sd[g] = ac.do(A.activation(RSTD[:, gslice(g)], MV[:, gslice(g), 1], ACT.Sqrt, bias=eps_col[:]))

            def invert(g, _):
                ve.after(sd[g])
                t = ve.do(V.reciprocal(RSTD[:, gslice(g)], RSTD[:, gslice(g)]))
                ve.after(t)
                iv[g] = ve.do(V.scalar_tensor_tensor(NMR[:, gslice(g)], MV[:, gslice(g), 0], -1.0, RSTD[:, gslice(g)],
                                                     ALU.mult, ALU.mult))

            def normalise(g, _):
                ac.after(iv[g])
                for j in gtiles(g):
                    nm[g] = ac.do(A.activation(dst(j), src(j), ACT.Identity, bias=NMR[:, j:j + 1], scale=RSTD[:, j:j + 1]))
            return [stats, deviation, invert, normalise]

        junk = []

        def norms(which, src, width, before, rn):
            sq, f2, rt = {}, {}, {}

            def squares(g, acc_point):
                ac.after(before(g, acc_point))
                for j in gtiles(g):
                    if len(junk) >= 4:
                        ac.after(junk[-4])
                    sq[g] = ac.do(A.activation(JUNK[:, len(junk) % 4, 0:width], src(j), ACT.Square,
                                               accum_out=SS[:, which, j:j + 1]))
                    junk.append(sq[g])

            def floor(g, _):
                ve.after(sq[g])
                f2[g] = ve.do(V.tensor_scalar(NRM[:, which, gslice(g)], SS[:, which, gslice(g)], NORM_EPS2, None, ALU.max))

            def root(g, _):
                ac.after(f2[g])
                rt[g] = ac.do(A.activation(NRM[:, which, gslice(g)], NRM[:, which, gslice(g)], ACT.Sqrt))

            def inverse(g, _):
                ve.after(rt[g])
                rn[g] = ve.do(V.reciprocal(RN[:, which, gslice(g)], NRM[:, which, gslice(g)]))
            return [squares, floor, root, inverse]

        def h_norm(conv, g):
            t = ve.do(V.tensor_tensor(HN[:, conv, gslice(g)], SS[:, 2, gslice(g)], RN[:, 2, gslice(g)], ALU.mult))
            ve.after(t)
            ve.do(V.tensor_scalar(HN[:, conv, gslice(g)], HN[:, conv, gslice(g)], scal[:, 1 + conv:2 + conv], None, ALU.mult))

        def scale_acc(pt, g, width, conv, before):
            ve.after(before)
            t = ve.do(V.tensor_tensor(RN[:, 0, gslice(g)], RN[:, 0, gslice(g)], HN[:, conv, gslice(g)], ALU.mult))
            ve.after(t)
            for j in gtiles(g):
                pt[g] = ve.do(V.tensor_scalar(ACC3[:, j, 0:width], ACC3[:, j, 0:width], RN[:, 0, j:j + 1], None, ALU.mult))

        class Store:

            def __init__(self, name):
                self.loads = [Loads(sem, f"store_{name}_{k}") for k in range(2)]
                self.pt = {}

            def put(self, g, dst, src, before):
                sp.after(before, self.pt.get(g - 2))
                self.pt[g] = self.loads[g % 2].add(S.dma_start(dst, src))

            @property
            def points(self):
                return [x.point for x in self.loads]

        def normed_rows(pt, g, src, width, table, store, *before):
            ve.after(*before)
            for j in gtiles(g):
                pt[g] = ve.do(V.tensor_scalar(ACC3[:, j, 0:width], src(j), RN[:, 2, j:j + 1], None, ALU.mult))
            store.put(g, table_rows(table, g), ACC3[:, gslice(g), 0:width], pt[g])

        def next_stage(name, *points):
            ends = (pe.last, ve.last, ac.last)
            for e in engines:
                e.after(*ends, *points)
            for e in (pe, ve, ac):
                e.stage(name)

        points = lambda names: [{} for _ in names.split()]

        def gather_pass(steps, table, width, arrived):
            for i in range(len(arrived), AHEAD - 1):
                arrived[i] = gather(i, table, width)
            for s in range(STEPS):
                steps.step(s)
                i = s + AHEAD - 1
                if i < N_ET and i not in arrived:
                    po.after(steps.product[max(s - 1, 0)], arrived.get(i - AHEAD))
                    arrived[i] = gather(i, table, width)

        def program(regular):
            next_stage("l0", xload.point, wload.point, tables, src3_stored.point, mask_stored.point, bases.point)
            t = ve.do(V.tensor_scalar(one_eps[:], scal[:, 0:1], 1.0, None, ALU.add))
            ac.after(t)
            for g in range(NG):
                acc0 = ac.do(A.mul(ACC3[:, gslice(g), 0:H], X[:, gslice(g), :], one_eps[:, 0:1]))
                xb2 = ve.do(V.tensor_tensor(AUX3[:, gslice(g), :], X[:, gslice(g), :], spread(b2_0, GROUPS[g], H), ALU.add))
            tr, cp, mm, re, m2, hb, st, sd, iv, nm, ga, s2, d2, i2, n2, rn, tb = points(
                "tr cp mm re m2 hb st sd iv nm ga s2 d2 i2 n2 rn tb")
            store_l1a = Store("l1a")

            def gin_first_product(g, _, mm=mm, cp=cp):
                pe.after(cp[g])
                for b, q, n in parts(g, 4):
                    mm[g] = pe.do(T.matmul(bank[HIGH[b]][:, 0:n * P], w1t0[:], ZT[:, q * P:(q + n) * P], start=True, stop=True))

            def relu_bias(mm, re, bias):
                def stage(g, _):
                    ac.after(mm[g])
                    for b, q, n in parts(g, 4):
                        re[g] = ac.do(A.activation(HT[:, q * P:(q + n) * P], bank[HIGH[b]][:, 0:n * P], ACT.Relu, bias=bias[:]))
                return stage

            def gin_residual(g, _, m2=m2, hb=hb):
                ve.after(m2[g], xb2)
                for b, q, n in parts(g, 4):
                    v = AUX3[:, START[g] + q:START[g] + q + n, :]
                    hb[g] = ve.do(V.tensor_tensor(v, wide(bank[LOW[b]][:, 0:n * H], H), v, ALU.add))

            def gin_affine(g, _, nm=nm, ga=ga):
                v = AUX3[:, gslice(g), :]
                ve.after(nm[g])
                t = ve.do(V.tensor_tensor(v, v, spread(gam, GROUPS[g], H), ALU.mult))
                ve.after(t)
                t = ve.do(V.tensor_tensor(v, v, spread(bet, GROUPS[g], H), ALU.add))
                ve.after(t)
                ga[g] = ve.do(V.scalar_tensor_tensor(v, v, 0.0, X[:, gslice(g), :], ALU.max, ALU.add))

            def l1a_table(g, _, rn=rn, tb=tb):
                ve.after(rn[g])
                h_norm(0, g)
                normed_rows(tb, g, xt, H, tab["l1a"], store_l1a)

            arrived = dict(first)
            steps = Steps(regular, LOC, H, (0, 1, 2, 3), arrived, acc0)
            steps.node_work([
                lambda g, acc, tr=tr: transposes(tr, g, at(H), H, LOW, acc),
                lambda g, _, tr=tr, cp=cp: copy_out(cp, g, ZT, H, LOW, tr[g]),
                gin_first_product,
                relu_bias(mm, re, b1_0),
                lambda g, _, m2=m2, re=re: products(m2, g, blocks(HT), [w2t0[:]], H, LOW, re[g]),
                gin_residual,
                *layer_norm(aux, aux, hb, st, sd, iv, nm),
                gin_affine,
                *layer_norm(aux, xt, ga, s2, d2, i2, n2),
                *norms(2, xt, H, lambda g, _, n2=n2: n2[g], rn),
                l1a_table])
            gather_pass(steps, tab["l0"], H, arrived)
            steps.finish()

            next_stage("l1a", *store_l1a.points)
            xtr, xcp, rn, sc, tr, cp, mm, ob, io, re, htr, ih, tb, hcp, hm, hb = points(
                "xtr xcp rn sc tr cp mm ob io re htr ih tb hcp hm hb")
            store_l1b, store_hw = Store("l1b"), Store("h1wr1")

            def sage_products(g, _, cp=cp, mm=mm, xcp=xcp):
                products(mm, g, lambda q: [ZT[:, q * P:(q + 1) * P], aux(START[g] + q)], [wl0[:], wr0[:]], H2, NODE_BANKS,
                         cp[g], xcp[g])

            def sage_bias(g, _, mm=mm, ob=ob):
                ve.after(mm[g])
                for b, q, n in parts(g, 2):
                    j = START[g] + q
                    ob[g] = ve.do(V.tensor_tensor(ACC3[:, j:j + n, 0:H2], wide(bank[NODE_BANKS[b]][:, 0:n * H2], H2),
                                                  spread(bl0, n, H2), ALU.add))

            def sage_relu(g, _, io=io, re=re):
                ac.after(io[g])
                for j in gtiles(g):
                    re[g] = ac.do(A.activation(ACC3[:, j, 0:H2], ACC3[:, j, 0:H2], ACT.Relu, scale=RN[:, 1, j:j + 1]))

            def l1b_table(g, _, ih=ih, tb=tb, htr=htr):
                ve.after(ih[g])
                h_norm(1, g)
                normed_rows(tb, g, at(H2), H2, tab["l1b"], store_l1b, htr[g])

            def h1_wr1_bias(g, _, hm=hm, hb=hb):
                ve.after(hm[g], store_hw.pt.get(g - 1))
                for b, q, n in parts(g, 4):
                    hb[g] = ve.do(V.tensor_tensor(wide(HT[:, q * H:(q + n) * H], H), wide(bank[LOW[b]][:, 0:n * H], H),
                                                  spread(bl1, n, H), ALU.add))
                store_hw.put(g, table_rows(aux1_dram, g), wide(HT[:, 0:GROUPS[g] * H], H), hb[g])

            arrived = {}
            steps = Steps(regular, LOC, H, (0, 1, 2, 3), arrived, None)
            steps.node_work([
                *norms(0, at(H), H, lambda g, acc: acc, rn),
                lambda g, _, sc=sc, rn=rn: scale_acc(sc, g, H, 0, rn[g]),
                lambda g, _, tr=tr, sc=sc: transposes(tr, g, at(H), H, LOW, sc[g]),
                lambda g, _, tr=tr, cp=cp: copy_out(cp, g, ZT, H, LOW, tr[g]),
                sage_products, sage_bias,
                *norms(1, at(H2), H2, lambda g, _, ob=ob: ob[g], io),
                sage_relu,
                lambda g, _, htr=htr, re=re: transposes(htr, g, at(H2), H2, NODE_BANKS, re[g]),
                *norms(2, at(H2), H2, lambda g, _, re=re: re[g], ih),
                l1b_table,
                lambda g, _, hcp=hcp, htr=htr: copy_out(hcp, g, ZT, H2, NODE_BANKS, htr[g]),
                lambda g, _, hm=hm, hcp=hcp: products(hm, g, blocks(ZT, 2), [wr1[:, 0, :], wr1[:, 1, :]], H, LOW, hcp[g]),
                h1_wr1_bias])
            for g in range(NG):
                banks = (LOW, HIGH)[g % 2]
                transposes(xtr, g, xt, H, banks, xcp.get(g - 2))
                copy_out_aux(xcp, g, banks, xtr[g])
            gather_pass(steps, tab["l1a"], H, arrived)
            steps.finish()

            next_stage("l1b", *store_l1b.points, *store_hw.points)
            rn, sc, tr, cp, mm, rl, ob, io, re, st, sd, iv, nm, xtr, xcp, tm, ts = points(
                "rn sc tr cp mm rl ob io re st sd iv nm xtr xcp tm ts")
            store_l2 = Store("l2")
            hw_load = [Loads(sem, f"load_h1wr1_{k}") for k in range(2)]
            R3 = wide(HT[:, 0:GMAX * H], H)
            O3 = wide(HT[:, GMAX * H:], H)
            r3 = lambda j: R3[:, j - max(x for x in START if x <= j), :]

            def second_load(g, _, rl=rl, nm=nm):
                sp.after(nm.get(g - 1))
                rl[g] = hw_load[g % 2].add(S.dma_start(R3[:, 0:GROUPS[g], :], table_rows(aux1_dram, g)))

            def second_bias(g, _, mm=mm, ob=ob, rl=rl):
                ve.after(mm[g], rl[g])
                for b, q, n in parts(g, 4):
                    ob[g] = ve.do(V.tensor_tensor(R3[:, q:q + n, :], wide(bank[LOW[b]][:, 0:n * H], H), R3[:, q:q + n, :],
                                                  ALU.add))

            def second_residual(g, _, io=io, re=re):
                ve.after(io[g])
                for j in gtiles(g):
                    re[g] = ve.do(V.scalar_tensor_tensor(r3(j), r3(j), RN[:, 1, j:j + 1], xt(j), ALU.mult, ALU.add))

            def message_parts(g, _, tm=tm, ts=ts):
                ve.after(tm[g], store_l2.pt.get(g - 1))
                for b, q, n in parts(g, 2):
                    j = START[g] + q
                    both = wide(bank[NODE_BANKS[b]][:, 0:n * H2], H2)
                    ve.do(V.tensor_tensor(ACC3[:, j:j + n, 0:H], both[:, :, 0:H], spread(bm, n, H), ALU.add))
                    ts[g] = ve.do(V.tensor_copy(O3[:, q:q + n, :], both[:, :, H:H2]))
                store_l2.put(g, table_rows(tab["l2"], g), O3[:, 0:GROUPS[g], :], ts[g])

            aux_blocks = lambda g: lambda q: [aux(START[g] + q)]
            arrived = {}
            steps = Steps(regular, LOC, H2, (0, 1, 2, 3), arrived, None)
            steps.node_work([
                *norms(0, at(H2), H2, lambda g, acc: acc, rn),
                lambda g, _, sc=sc, rn=rn: scale_acc(sc, g, H2, 1, rn[g]),
                second_load,
                lambda g, _, tr=tr, sc=sc: transposes(tr, g, at(H2), H2, NODE_BANKS, sc[g]),
                lambda g, _, tr=tr, cp=cp: copy_out(cp, g, ZT, H2, NODE_BANKS, tr[g]),
                lambda g, _, mm=mm, cp=cp: products(mm, g, blocks(ZT, 2), [wl1[:, 0, :], wl1[:, 1, :]], H, LOW, cp[g]),
                second_bias,
                *norms(1, r3, H, lambda g, _, ob=ob: ob[g], io),
                second_residual,
                *layer_norm(r3, xt, re, st, sd, iv, nm),
                lambda g, _, xtr=xtr, nm=nm: transposes(xtr, g, xt, H, HIGH, nm[g]),
                lambda g, _, xtr=xtr, xcp=xcp: copy_out_aux(xcp, g, HIGH, xtr[g]),
                lambda g, _, tm=tm, xcp=xcp: products(tm, g, aux_blocks(g), [wms[:, :, :].rearrange("p k h -> p (k h)")], H2,
                                                      NODE_BANKS, xcp[g]),
                message_parts])
            gather_pass(steps, tab["l1b"], H2, arrived)
            steps.finish()

            next_stage("l2", *store_l2.points)
            CH = 4
            NCH = -(-N_ET // CH)
            TURN, BACK = 2, 3
            SCAN = [JUNK[:, 2 * k:2 * k + 2, :].rearrange("p a b -> p (a b)") for k in range(2)]
            acc0 = ve.do(V.memset(ACC3[:, :, H:H + 1], 0.0))
            ones_ready = ve.do(V.memset(RG3[:, :, H:H + 1], 1.0))
            mask_loads = [Loads(sem, f"load_mask_{k}") for k in range(2)]
            arrived, messages, m_ready, turned, scanned, back, loaded = ({} for _ in range(7))
            tiles_of = lambda c: range(c * CH, min((c + 1) * CH, N_ET))
            steps = Steps(regular, LOCEND, H + 1, (0, 1), m_ready, acc0)

            def load_mask(c):
                if c < NCH:
                    sp.after(scanned.get(c - 2))
                    loaded[c] = mask_loads[c % 2].add(S.dma_start(
                        MASK[:, c % 2, :], mask_dram[0:1, c * 512:(c + 1) * 512].to_broadcast([P, 512])))

            def message(i):
                if i < N_ET:
                    ve.after(arrived[i])
                    rows = RG3[:, i % RING, UP:UP + H]
                    messages[i] = ve.do(V.scalar_tensor_tensor(rows, ww[:], WEIGHT[:, i:i + 1], rows, ALU.mult, ALU.add))

            def turn(c):
                pe.after(messages[tiles_of(c)[-1]], scanned.get(c - 1))
                for q, i in enumerate(tiles_of(c)):
                    turned[c] = pe.do(T.transpose(bank[TURN][:, q * P:(q + 1) * P], RG3[:, i % RING, UP:UP + H], IDENT))

            def scan(c):
                n = len(tiles_of(c)) * P
                ve.after(turned[c], loaded[c], back.get(c - 2), scanned.get(c - 1))
                scanned[c] = ve.do(V.tensor_tensor_scan(SCAN[c % 2][:, 0:n], MASK[:, c % 2, 0:n], bank[TURN][:, 0:n],
                                                        SCAN[(c - 1) % 2][:, 511:512] if c else -BIG, ALU.min, ALU.max))

            def turn_back(c):
                n = len(tiles_of(c))
                pe.after(scanned[c], m_ready.get(c * CH - 1))
                for q in range(n):
                    back[c] = pe.do(T.transpose(bank[BACK][:, q * P:(q + 1) * P], SCAN[c % 2][:, q * P:(q + 1) * P], IDENT))
                freeing = c * CH + CH - 1 - AHEAD
                ac.after(back[c], steps.product[freeing] if freeing >= 0 else None, ones_ready)
                slot = (c * CH) % RING
                t = ac.do(A.copy(RG3[:, slot:slot + n, 0:H], wide(bank[BACK][:, 0:n * P], P)))
                for i in tiles_of(c):
                    m_ready[i] = t

            hs, tr, cp, mm, re, m2, ob, st, sd, iv, nm, xtr, xcp, tm, ts = points(
                "hs tr cp mm re m2 ob st sd iv nm xtr xcp tm ts")
            store_l3 = Store("l3")

            def present(g, acc, hs=hs):
                ve.after(acc)
                for j in gtiles(g):
                    hs[g] = ve.do(V.tensor_scalar(at(H)(j), at(H)(j), ACC3[:, j, H:H + 1], None, ALU.mult))

            def max_first_product(g, _, cp=cp, mm=mm):
                pe.after(cp[g])
                for b, q, n in parts(g, 4):
                    o = bank[HIGH[b]][:, 0:n * P]
                    pe.do(T.matmul(o, w1_2[:, 0, :], AUX3[:, START[g] + q:START[g] + q + n, :], start=True, stop=False))
                    mm[g] = pe.do(T.matmul(o, w1_2[:, 1, :], ZT[:, q * P:(q + n) * P], start=False, stop=True))

            def max_residual(g, _, m2=m2, ob=ob):
                ve.after(m2[g])
                for b, q, n in parts(g, 4):
                    t = ve.do(V.tensor_tensor(ACC3[:, START[g] + q:START[g] + q + n, 0:H], wide(bank[LOW[b]][:, 0:n * H], H),
                                              spread(b2_2, n, H), ALU.add))
                ve.after(t)
                v = ACC3[:, gslice(g), 0:H]
                ob[g] = ve.do(V.tensor_tensor(v, v, X[:, gslice(g), :], ALU.add))

            def l3_table(g, _, tm=tm, ts=ts, m2=m2):
                ve.after(tm[g], m2[g], store_l3.pt.get(g - 1))
                o = wide(HT[:, :], H2)
                for b, q, n in parts(g, 2):
                    ts[g] = ve.do(V.tensor_tensor(o[:, q:q + n, :], wide(bank[NODE_BANKS[b]][:, 0:n * H2], H2),
                                                  spread(bdc, n, H2), ALU.add))
                store_l3.put(g, table_rows(tab["l3"], g, 2), o[:, 0:GROUPS[g], :], ts[g])

            steps.node_work([
                present,
                lambda g, _, tr=tr, hs=hs: transposes(tr, g, at(H), H, LOW, hs[g]),
                lambda g, _, tr=tr, cp=cp: copy_out(cp, g, ZT, H, LOW, tr[g]),
                max_first_product,
                lambda g, _, mm=mm, re=re: (ac.after(store_l3.pt.get(g - 1)), relu_bias(mm, re, b1_2)(g, _)),
                lambda g, _, m2=m2, re=re: products(m2, g, blocks(HT), [w2_2[:]], H, LOW, re[g]),
                max_residual,
                *layer_norm(at(H), xt, ob, st, sd, iv, nm),
                lambda g, _, xtr=xtr, nm=nm: transposes(xtr, g, xt, H, HIGH, nm[g]),
                lambda g, _, xtr=xtr, xcp=xcp: copy_out_aux(xcp, g, HIGH, xtr[g]),
                lambda g, _, tm=tm, xcp=xcp: products(tm, g, aux_blocks(g), [wdc[:, :, :].rearrange("p k h -> p (k h)")], H2,
                                                      NODE_BANKS, xcp[g]),
                l3_table])
            load_mask(0)
            load_mask(1)
            for i in range(AHEAD):
                arrived[i] = gather(i, tab["l2"], H, UP)
            done = 0

            def steps_before(tile, done, most=STEPS):
                end = min(STEPS, done + most)
                while done < end and (NEWEST[done] if regular else min(done, N_ET - 1)) < tile:
                    steps.step(done)
                    done += 1
                return done

            def ahead(c):
                for i in range(c * CH, min((c + 1) * CH, N_ET)):
                    po.after(messages[i - AHEAD], turned.get((i - RING) // CH))
                    arrived[i] = gather(i, tab["l2"], H, UP)

            for i in range(2 * CH):
                message(i)
            for c in range(AHEAD // CH, AHEAD // CH + 2):
                ahead(c)
            turn(0)
            for c in range(NCH):
                scan(c)
                load_mask(c + 2)
                message((c + 2) * CH)
                done = steps_before(c * CH, done, 1)
                message((c + 2) * CH + 1)
                done = steps_before(c * CH, done, 1)
                if c + 1 < NCH:
                    turn(c + 1)
                message((c + 2) * CH + 2)
                done = steps_before(c * CH, done, 1)
                message((c + 2) * CH + 3)
                turn_back(c)
                ahead(c + 2 + AHEAD // CH)
                done = steps_before(c * CH, done)
            done = steps_before(N_ET, done)
            src3_load = Loads(sem, "load_src3")
            sp.after(*[g.point for g in gathered])
            src3_load.add(S.dma_start(SRC[:], src3_dram))
            steps.finish()

            next_stage("l3", *store_l3.points, src3_load.point)
            sm, sa, re, st, sd, iv, nm = points("sm sa re st sd iv nm")
            store_out = Store("out")
            for g in range(NG):
                banks = (LOW, HIGH)[g % 2]
                products(sm, g, aux_blocks(g), [wst[:]], H, banks, sa.get(g - 2))
                ve.after(sm[g])
                for b, q, n in parts(g, 4):
                    j = START[g] + q
                    sa[g] = ve.do(V.tensor_tensor(ACC3[:, j:j + n, 0:H], wide(bank[banks[b]][:, 0:n * H], H),
                                                  spread(bs, n, H), ALU.add))

            def relational_residual(g, acc, re=re):
                v = ACC3[:, gslice(g), 0:H]
                ve.after(acc)
                re[g] = ve.do(V.scalar_tensor_tensor(v, v, 0.0, X[:, gslice(g), :], ALU.max, ALU.add))

            def result(g, _, nm=nm):
                full = min(START[g + 1], N // P)
                store_out.put(g, out[START[g] * P:full * P, :].rearrange("(t p) c -> p t c", p=P), X[:, START[g]:full, :],
                              nm[g])
                if full < START[g + 1]:
                    store_out.loads[g % 2].add(S.dma_start(out[full * P:N, :], X[0:N % P, NT - 1, :]))

            arrived = {}
            steps = Steps(regular, LOC, H, (0, 1, 2, 3), arrived, sa[NG - 1])
            steps.node_work([relational_residual, *layer_norm(at(H), xt, re, st, sd, iv, nm), result])
            gather_pass(steps, tab["l3"], H, arrived)
            steps.finish()
            sp.after(*store_out.points)

        for e in engines:
            e.after(flag_ready)
        irregular = nc.values_load(FLAG[0:1, 0:1], min_val=0, max_val=2 * ROWS * P)
        state = [dict(e.waited) for e in engines], [g.count for g in gathered], [e.last for e in engines]

        def restart():
            for e, waited, last in zip(engines, state[0], state[2]):
                e.waited, e.last = dict(waited), last
            for g, count in zip(gathered, state[1]):
                g.count = count

        with nc.If(irregular == 0):
            restart()
            program(True)
        with nc.Else():
            restart()
            program(False)


def kernel(**k):
    import concourse.bacc as bacc
    from concourse.bass_utils import run_bass_kernel_spmd as run

    def padded(v, n, fill):
        v = np.asarray(v)
        return np.concatenate([v, np.full((n - v.shape[0],) + v.shape[1:], fill, v.dtype)])

    src, dst = np.asarray(k["src"]), np.asarray(k["dst"])
    tiles = lambda v: padded(v, N_ET * P, 0).reshape(N_ET, P).T
    edge_rows = lambda v: padded(v, ROWS * P, NO_NODE).reshape(ROWS, P)
    consts = np.zeros((P, 3 * P + 2 * SC + 1 + NT), np.float32)
    consts[:, 0:P] = np.eye(P)
    consts[:, P:2 * P] = np.eye(P, k=1)
    consts[:, 2 * P:3 * P] = np.arange(P)
    consts[:, 3 * P:3 * P + SC] = np.arange(SC)[None, :] * P + np.arange(P)[:, None]
    consts[:, 3 * P + SC] = P * (np.arange(P) + 1)
    never = float(2 * ROWS)
    consts[:, 3 * P + SC + 1:3 * P + 2 * SC + 1] = np.array(NEWEST + [never] * (ROWS - STEPS)).reshape(SC, P).T
    consts[:, 3 * P + 2 * SC + 1:] = [DONE_BY[START.index(t + 1) - 1] if t + 1 in START else never for t in range(NT)]
    r = lambda name: np.asarray(k[name]).reshape(1, -1)
    arrays = {
        "x": padded(k["x"], NP, 0), "src_cols": tiles(src), "type_cols": tiles(k["edge_type_2"]),
        "dst_rows": edge_rows(dst), "next_rows": edge_rows(dst[1:]),
        "prev_rows": edge_rows(np.concatenate([np.full(1, NO_NODE, dst.dtype), dst])),
        "weight_cols": tiles(k["edge_weight"]), "consts": consts,
        "l0_w1t": k["L0_gnn_W1"].T, "l0_w2t": k["L0_gnn_W2"].T, "l0_b1": r("L0_gnn_b1"), "l0_b2": r("L0_gnn_b2"),
        "l0_gamma": r("L0_gnn_gamma"), "l0_beta": r("L0_gnn_beta"), "l0_eps": r("L0_gnn_eps"),
        "l1_scale0": r("L1_gnn_scale0"), "l1_scale1": r("L1_gnn_scale1"),
        "l1_wl0": k["L1_gnn_Wl0"], "l1_wr0": k["L1_gnn_Wr0"], "l1_wl1": k["L1_gnn_Wl1"], "l1_wr1": k["L1_gnn_Wr1"],
        "l1_bl0": r("L1_gnn_bl0"), "l1_bl1": r("L1_gnn_bl1"),
        "l2_wm": k["L2_gnn_Wm"], "l2_bm": r("L2_gnn_bm"), "l2_w1": k["L2_gnn_W1"], "l2_b1": r("L2_gnn_b1"),
        "l2_w2": k["L2_gnn_W2"], "l2_b2": r("L2_gnn_b2"),
        "l3_wdt": k["L3_gnn_W_data"].T, "l3_wct": k["L3_gnn_W_control"].T, "l3_wst": k["L3_gnn_W_self"].T,
        "l3_bd": r("L3_gnn_b_data"), "l3_bc": r("L3_gnn_b_control"), "l3_bs": r("L3_gnn_b_self"),
    }
    arrays = {n: np.ascontiguousarray(v) for n, v in arrays.items()}
    nc = bacc.Bacc("TRN2", target_bir_lowering=False, num_devices=1)
    a = {n: nc.dram_tensor(f"in_{n}", v.shape, mybir.dt.from_np(v.dtype), kind="ExternalInput").ap() for n, v in arrays.items()}
    out = nc.dram_tensor("out", (N, H), F32, kind="ExternalOutput").ap()
    build(nc, a, out)
    return run(nc, [{f"in_{n}": v for n, v in arrays.items()}], core_ids=[0]).results[0]["out"]
```

```python
from contextlib import ExitStack
from itertools import zip_longest

import numpy as np

import concourse.bass as bass
from concourse import mybir

F32 = mybir.dt.float32
BF16 = mybir.dt.bfloat16
I32 = mybir.dt.int32
AX_X = mybir.AxisListType.X
ALU = mybir.AluOpType
ACT = mybir.ActivationFunctionType

P = 128
H = 128
H2 = 256
N = 6250
E = 106250
NT = -(-N // P)
NP = NT * P
N_ET = -(-E // P)
STEPS = N_ET + NT - 1
SC = -(-STEPS // P)
ROWS = SC * P
LAG = NT - 1
RING = 64
SLOT = 264
UP = 136
AHEAD = RING - LAG
GROUPS = (8, 8, 8, 8, 8, 4, 3, 1, 1)
START = [sum(GROUPS[:g]) for g in range(len(GROUPS) + 1)]
NG = len(GROUPS)
GMAX = max(GROUPS)
OH_BATCH = 4
OH_RING = 3 * OH_BATCH
REGS = 8
NO_NODE = 8192
BIG = 3.3895313892515355e38
LN_EPS = 1e-5
NORM_EPS2 = 1e-24
assert START[-1] == NT and AHEAD > 0 and ROWS >= N_ET and 2 * max(GROUPS[-2:]) <= GMAX
END_MARGIN, TILE_MARGIN = 6, 4
DONE_BY = [min(STEPS, -(-START[g + 1] * STEPS // NT) + END_MARGIN) for g in range(NG - 1)] + [STEPS]
NEWEST = [min(s, N_ET - 1, s * N_ET // STEPS + TILE_MARGIN) for s in range(STEPS)]
OLDEST = [max(0, s - (NT - 1), s * N_ET // STEPS - TILE_MARGIN) for s in range(STEPS)]


class Engine:

    def __init__(self, sem, eng, name):
        self.new_sem, self.eng, self.name = sem, eng, name
        self.waited = {}
        self.last = None

    def stage(self, stage):
        self.key = f"{self.name}_{stage}"
        self.sem, self.count = self.new_sem(self.key), 0

    def do(self, instruction):
        self.count += 1
        instruction.then_inc(self.sem, 1)
        self.last = (self.key, self.sem, self.count)
        return self.last

    def after(self, *points):
        for point in points:
            if point is None:
                continue
            key, sem, value = point
            if self.waited.get(key, 0) < value:
                self.waited[key] = value
                self.eng.wait_ge(sem, value)


class Loads:

    def __init__(self, sem, name):
        self.key, self.sem, self.count = name, sem(name), 0

    def add(self, instruction):
        self.count += 16
        instruction.then_inc(self.sem, 16)
        return (self.key, self.sem, self.count)

    @property
    def point(self):
        return (self.key, self.sem, self.count)


def build(nc, a, out):
    ctx = ExitStack()
    with ctx:
        def sb(name, shape, dt=F32):
            return ctx.enter_context(nc.sbuf_tensor(name, shape, dt))

        def dram(name, shape, dt=F32):
            return nc.dram_tensor(name, shape, dt, kind="Internal").ap()

        semaphores = {}

        def sem(name):
            if name not in semaphores:
                semaphores[name] = ctx.enter_context(nc.semaphore(name))
            return semaphores[name]

        pe, ve, ac, po, sp = engines = [Engine(sem, e, n) for e, n in (
            (nc.tensor, "pe"), (nc.vector, "ve"), (nc.scalar, "ac"), (nc.gpsimd, "po"), (nc.sync, "sp"))]
        V, A, T, G, S = nc.vector, nc.scalar, nc.tensor, nc.gpsimd, nc.sync
        for e in (pe, ve, ac):
            e.stage("prep")

        X = sb("x_nodes", [P, NT, H])
        ACC = sb("acc", [P, NT * SLOT])
        RG = sb("ring", [P, RING * SLOT])
        OH = sb("onehot", [P, OH_RING, P])
        LOC = sb("loc", [P, ROWS])
        LOCEND = sb("loc_end", [P, ROWS])
        SRC = sb("src_cols", [P, N_ET], I32)
        BASES = sb("bases", [2, ROWS], I32)
        CST = sb("consts", [P, 3 * P + 3 * SC + 1 + NT])
        ZT = sb("zt", [P, GMAX * H2])
        HT = sb("ht", [P, GMAX * H2])
        JUNK = sb("junk", [P, 4, H2])
        MASK = sb("mask", [P, 2, 512], BF16)
        WEIGHT = sb("edge_weights", [P, N_ET])
        FLAG = sb("irregular", [1, 1], I32)
        one_eps = sb("one_plus_eps", [P, 1])
        ST = sb("bn_parts", [P, GMAX, 6])
        MV = sb("mean_var", [P, NT, 2])
        RSTD = sb("rstd", [P, NT])
        NMR = sb("neg_mean_rstd", [P, NT])
        SS = sb("sumsq", [P, 3, NT])
        NRM = sb("norms", [P, 3, NT])
        RN = sb("rnorms", [P, 3, NT])
        HN = sb("h_norm", [P, 2, NT])
        IDENT, SHIFT2 = CST[:, 0:P], CST[:, 0:2 * P]
        IOTA = CST[:, 2 * P:3 * P]
        STEPNO, BOUND = CST[:, 3 * P:3 * P + SC], CST[:, 3 * P + SC:3 * P + SC + 1]
        AT_MOST = CST[:, 3 * P + SC + 1:3 * P + 2 * SC + 1]
        AT_LEAST = CST[:, 3 * P + 2 * SC + 1:3 * P + 3 * SC + 1]
        END_BY = CST[:, 3 * P + 3 * SC + 1:]
        ACC3 = ACC[:, :].rearrange("p (t c) -> p t c", c=SLOT)
        AUX3 = ACC3[:, :, UP:UP + H]
        RG3 = RG[:, :].rearrange("p (t c) -> p t c", c=SLOT)
        bank = [ctx.enter_context(nc.psum_tensor(f"bank{b}", [P, 512], F32)) for b in range(8)]

        wload = Loads(sem, "load_weights")

        def weight(name, src, shape):
            w = sb(name, shape)
            wload.add(S.dma_start(w[:], src))
            return w

        def row(name, *srcs):
            n = sum(s.shape[-1] for s in srcs)
            w, at = sb(name, [P, n]), 0
            for s in srcs:
                k = s.shape[-1]
                wload.add(S.dma_start(w[:, at:at + k], s.to_broadcast([P, k])))
                at += k
            return w

        xload = Loads(sem, "load_x")
        iload = Loads(sem, "load_indices")
        iload.add(S.dma_start(SRC[:], a["src_cols"]))
        DROWS = ZT[:, 0:ROWS].bitcast(I32).rearrange("p (c e) -> p c e", e=P)
        dload = Loads(sem, "load_dst")
        dload.add(S.dma_start(CST[:], a["consts"]))
        dload.add(S.dma_start(DROWS, a["dst_rows"].rearrange("(c p) e -> p c e", p=P)))
        TYPE = HT[:, 0:N_ET].bitcast(I32)
        DPREV = ZT[:, ROWS:2 * ROWS].bitcast(I32)
        tload = Loads(sem, "load_type_prev")
        tload.add(S.dma_start(TYPE, a["type_cols"]))
        tload.add(S.dma_start(DPREV.rearrange("p (c e) -> p c e", e=P),
                              a["prev_rows"].rearrange("(c p) e -> p c e", p=P)))
        for g in range(NG):
            tiles = slice(START[g], START[g + 1])
            xload.add(S.dma_start(X[:, tiles, :], a["x"].rearrange("(t p) h -> p t h", p=P)[:, tiles, :]))
        w1t0 = weight("l0_w1t", a["l0_w1t"], [P, H])
        w2t0 = weight("l0_w2t", a["l0_w2t"], [P, H])
        b1_0 = weight("l0_b1", a["l0_b1"].rearrange("o p -> p o"), [P, 1])
        b2_0, gam, bet = row("l0_b2", a["l0_b2"]), row("l0_gamma", a["l0_gamma"]), row("l0_beta", a["l0_beta"])
        scal = row("scalars", a["l0_eps"], a["l1_scale0"], a["l1_scale1"])
        wl0 = weight("l1_wl0", a["l1_wl0"], [P, H2])
        wr0 = weight("l1_wr0", a["l1_wr0"], [P, H2])
        bl0, bl1 = row("l1_bl0", a["l1_bl0"]), row("l1_bl1", a["l1_bl1"])
        wl1 = weight("l1_wl1", a["l1_wl1"].rearrange("(k p) h -> p k h", p=P), [P, 2, H])
        wr1 = weight("l1_wr1", a["l1_wr1"].rearrange("(k p) h -> p k h", p=P), [P, 2, H])
        wms = weight("l2_wm", a["l2_wm"][0:2 * H, :].rearrange("(k p) h -> p k h", p=P), [P, 2, H])
        ww = row("l2_ww", a["l2_wm"][2 * H:2 * H + 1, :])
        wload.add(S.dma_start(WEIGHT[:], a["weight_cols"]))
        bm = row("l2_bm", a["l2_bm"])
        w1_2 = weight("l2_w1", a["l2_w1"].rearrange("(k p) h -> p k h", p=P), [P, 2, H])
        b1_2 = weight("l2_b1", a["l2_b1"].rearrange("o p -> p o"), [P, 1])
        w2_2 = weight("l2_w2", a["l2_w2"], [P, H])
        b2_2 = row("l2_b2", a["l2_b2"])
        wdc = sb("l3_wdc", [P, 2, H])
        wload.add(S.dma_start(wdc[:, 0, :], a["l3_wdt"]))
        wload.add(S.dma_start(wdc[:, 1, :], a["l3_wct"]))
        bdc = row("l3_bdc", a["l3_bd"], a["l3_bc"])
        wst = weight("l3_wst", a["l3_wst"], [P, H])
        bs = row("l3_bs", a["l3_bs"])
        eps_col = sb("ln_eps", [P, 1])
        eps_ready = ve.do(V.memset(eps_col[:], LN_EPS))

        tab = {"l0": a["x"], "l1a": dram("tab_l1a", [NP, H]), "l1b": dram("tab_l1b", [NP, H2]),
               "l2": dram("tab_l2", [NP, H]), "l3": dram("tab_l3", [2 * NP, H])}
        mask_dram = dram("scan_mask", [1, ROWS * P], BF16)
        src3_dram = dram("src_type_cols", [P, N_ET], I32)
        aux1_dram = dram("h1_wr1", [NP, H])

        gathered = [Loads(sem, f"gathered{k}") for k in range(AHEAD)]

        def gather(i, table, width, at=0):
            return gathered[i % AHEAD].add(G.indirect_dma_start(
                RG3[:, i % RING, at:at + width], None, table, bass.IndirectOffsetOnAxis(ap=SRC[:, i:i + 1], axis=0)))

        first = {}

        def first_gathers(upto):
            for i in range(len(first), upto):
                po.after(first.get(i - AHEAD))
                first[i] = gather(i, tab["l0"], H)

        po.after(iload.point)
        first_gathers(10)

        W = ACC[:, :]
        col = lambda at, n=1: W[:, at:at + n]
        FIRST, CMP, TK, CNT = col(0, SC), col(16, SC * P), col(8), col(9)
        BK, BKI, FL, CE = col(10), col(11).bitcast(I32), col(12), col(13)
        TKI = col(14).bitcast(I32)
        ve.after(dload.point)
        t = ve.do(V.tensor_copy(FIRST, DROWS[:, :, 0]))
        ve.after(t)
        KROW = col(2000, P)
        t = ve.do(V.tensor_scalar(KROW, IOTA, 1.0, float(P), ALU.add, ALU.mult))
        ve.after(t)
        for c in range(SC):
            t = ve.do(V.tensor_scalar(CMP[:, c * P:(c + 1) * P], KROW, FIRST[:, c:c + 1], None, ALU.is_gt))
        ones = sb("ones", [P, 1])
        t = ve.do(V.memset(ones[:], 1.0))
        pe.after(t, dload.point)
        for c in range(SC):
            t = pe.do(T.matmul(bank[0][:, 0:1], CMP[:, c * P:(c + 1) * P], ones[:], start=c == 0, stop=c == SC - 1))
        ve.after(t)
        t = ve.do(V.tensor_scalar(TK, bank[0][:, 0:1], -1.0, 0.0, ALU.add, ALU.max))
        ve.after(t)
        t = ve.do(V.tensor_copy(TKI, TK))
        po.after(t)
        rows_of = Loads(sem, "gather_boundary_rows")
        BROWS = col(2200, P).bitcast(I32)
        rows_of.add(G.indirect_dma_start(BROWS, None, a["dst_rows"], bass.IndirectOffsetOnAxis(ap=TKI, axis=0)))
        first_gathers(32)
        ve.after(rows_of.point)
        BROWF = col(2400, P)
        t = ve.do(V.tensor_copy(BROWF, BROWS))
        ve.after(t)
        t = ve.do(V.tensor_scalar(col(2600, P), BROWF, BOUND, None, ALU.is_lt, ALU.add, accum_out=CNT))
        ve.after(t)
        t = ve.do(V.scalar_tensor_tensor(BK, TK, float(P), CNT, ALU.mult, ALU.add))
        ve.after(t)
        t = ve.do(V.tensor_copy(BKI, BK))
        ve.after(t)
        FLI, CEI, BPI = col(15).bitcast(I32), col(2800).bitcast(I32), col(2801).bitcast(I32)
        BP = col(2802)
        ve.do(V.tensor_scalar(FLI, BKI, 7, None, ALU.logical_shift_right))
        t = ve.do(V.tensor_scalar(BP, BK, float(P - 1), None, ALU.add))
        ve.after(t)
        t = ve.do(V.tensor_copy(BPI, BP))
        ve.after(t)
        t = ve.do(V.tensor_scalar(CEI, BPI, 7, None, ALU.logical_shift_right))
        ve.after(t)
        ve.do(V.tensor_copy(FL, FLI))
        t = ve.do(V.tensor_copy(CE, CEI))
        pe.after(t)
        for b, v in ((1, BK), (2, FL), (3, CE)):
            t = pe.do(T.matmul(bank[b][:, 0:2 * P], v.to_broadcast([P, P]), SHIFT2, start=True, stop=True))
        ve.after(t)
        ROWB, ROWF, ROWC = col(3000, 2 * P), col(3300, 2 * P), col(3600, 2 * P)
        for b, v in ((1, ROWB), (2, ROWF), (3, ROWC)):
            t = ve.do(V.tensor_copy(v, bank[b][:, 0:2 * P]))
        ve.after(t)
        NOTEMPTY, NSTEP, TEND, DIFF = col(3900, NT), col(3960, NT), col(4020, NT), col(4080, NT)
        ONEROW = col(4140, NT)
        ve.do(V.tensor_tensor(NOTEMPTY, ROWB[:, 0:NT], ROWB[:, P:P + NT], ALU.is_gt))
        ve.do(V.tensor_tensor(NSTEP, ROWC[:, 0:NT], ROWF[:, P:P + NT], ALU.subtract))
        ve.do(V.memset(ONEROW, 1.0))
        t = ve.do(V.tensor_tensor(DIFF, ROWF[:, 0:NT], ROWF[:, P:P + NT], ALU.subtract))
        ve.after(t)
        t = ve.do(V.tensor_tensor(NSTEP, NSTEP, NOTEMPTY, ALU.mult))
        ve.after(t)
        ve.do(V.tensor_tensor_scan(TEND, ONEROW, NSTEP, 0.0, ALU.mult, ALU.add))
        t = ve.do(V.tensor_tensor(DIFF, DIFF, NSTEP, ALU.subtract))
        ve.after(t)
        JS, IS, JC, SUB = col(4200, SC), col(4210, SC), col(4220, SC), col(4230, SC)
        ISUM = col(4240, SC)
        for c in range(SC):
            GE = col(4300 + 64 * c, NT)
            t = ve.do(V.tensor_scalar(GE, TEND, STEPNO[:, c:c + 1], None, ALU.is_le, ALU.add, accum_out=JS[:, c:c + 1]))
            ve.after(t)
            t = ve.do(V.tensor_tensor_reduce(out=col(4800 + 64 * c, NT), in0=GE, in1=DIFF, scale=1.0, scalar=0.0,
                                             op0=ALU.mult, op1=ALU.add, accum_out=ISUM[:, c:c + 1]))
        ve.after(t)
        t = ve.do(V.tensor_tensor(IS, ISUM, STEPNO, ALU.add))
        ve.after(t)
        ISF, ISI = col(5300, SC), col(5310, SC).bitcast(I32)
        ve.do(V.tensor_scalar(ISF, IS, float(N_ET - 1), None, ALU.min))
        ve.do(V.tensor_scalar(JC, JS, float(NT - 1), float(SLOT), ALU.min, ALU.mult))
        t = ve.do(V.tensor_scalar(SUB, JS, float(P), None, ALU.mult))
        ve.after(t)
        is_ready = ve.do(V.tensor_copy(ISI, ISF))
        po.after(is_ready)
        DCUR, DNXT = col(5400, ROWS).bitcast(I32), col(6300, ROWS).bitcast(I32)
        step_rows = Loads(sem, "gather_step_rows")
        for c in range(SC):
            for rows, src in ((DCUR, a["dst_rows"]), (DNXT, a["next_rows"])):
                step_rows.add(G.indirect_dma_start(rows[:, c * P:(c + 1) * P], None, src,
                                                   bass.IndirectOffsetOnAxis(ap=ISI[:, c:c + 1], axis=0)))
        first_gathers(RING)
        OFF, LATE, BAD = col(12830, 2 * SC), col(12850, NT), col(12900, 2)
        ve.after(is_ready)
        ve.do(V.tensor_tensor(OFF[:, 0:SC], ISF, AT_MOST, ALU.is_gt))
        ve.do(V.tensor_tensor(OFF[:, SC:2 * SC], ISF, AT_LEAST, ALU.is_lt))
        t = ve.do(V.tensor_tensor(LATE, TEND, END_BY, ALU.is_gt))
        ve.after(t)
        ve.do(V.tensor_reduce(BAD[:, 0:1], OFF, AX_X, ALU.add))
        t = ve.do(V.tensor_reduce(BAD[:, 1:2], LATE, AX_X, ALU.add))
        ve.after(t)
        BADSUM = col(12910)
        t = ve.do(V.tensor_tensor(BADSUM, BAD[:, 0:1], BAD[:, 1:2], ALU.add))
        pe.after(t)
        t = pe.do(T.matmul(bank[5][0:1, 0:1], BADSUM, ones[:], start=True, stop=True))
        ve.after(t)
        flag_ready = ve.do(V.tensor_copy(FLAG[:], bank[5][0:1, 0:1]))
        ve.after(is_ready)
        SLI, SLF = col(5320, SC).bitcast(I32), col(5330, 2 * SC)
        t = ve.do(V.tensor_scalar(SLI, ISI, RING - 1, None, ALU.bitwise_and))
        ve.after(t)
        ve.do(V.tensor_scalar(SLF[:, 0:SC], SLI, float(SLOT), None, ALU.mult))
        t = ve.do(V.tensor_copy(SLF[:, SC:2 * SC], JC))
        pe.after(t)
        pe.do(T.transpose(bank[4][0:SC, 0:P], SLF[:, 0:SC], IDENT))
        t = pe.do(T.transpose(bank[4][0:SC, P:2 * P], SLF[:, SC:2 * SC], IDENT))
        ve.after(t)
        BROW2 = W[0:SC, 7200:7200 + 2 * P].bitcast(I32)
        t = ve.do(V.tensor_copy(BROW2, bank[4][0:SC, 0:2 * P]))
        sp.after(t)
        bases = Loads(sem, "move_bases")
        for n in range(2):
            bases.add(S.dma_start(BASES[n:n + 1, :], BROW2[:, n * P:(n + 1) * P]))
        ve.after(tload.point, iload.point)
        SRC3 = col(12000, N_ET).bitcast(I32)
        t = ve.do(V.scalar_tensor_tensor(SRC3, SRC[:], 2.0, TYPE, ALU.mult, ALU.add))
        sp.after(t)
        src3_stored = Loads(sem, "store_src3")
        src3_stored.add(S.dma_start(src3_dram, SRC3))
        NEQ = col(7500, ROWS)
        t = ve.do(V.tensor_tensor(NEQ, ZT[:, 0:ROWS].bitcast(I32), DPREV, ALU.not_equal))
        ve.after(t)
        t = ve.do(V.tensor_scalar(NEQ, NEQ, -2.0, 1.0, ALU.mult, ALU.add))
        ve.after(t)
        MASKV = col(8400, ROWS // 2).bitcast(BF16)
        t = ve.do(V.tensor_scalar(MASKV, NEQ, BIG, None, ALU.mult))
        sp.after(t)
        mask_stored = Loads(sem, "store_mask")
        mask_stored.add(S.dma_start(mask_dram.rearrange("o (c p e) -> (o p) c e", p=P, e=P),
                                    MASKV.rearrange("p (c e) -> p c e", e=P)))
        ve.after(step_rows.point)
        LC, LE = col(8900, ROWS), col(9800, ROWS)
        NE = col(10700, ROWS)
        for c in range(SC):
            ve.do(V.tensor_scalar(LC[:, c * P:(c + 1) * P], DCUR[:, c * P:(c + 1) * P], SUB[:, c:c + 1], None,
                                  ALU.subtract))
        t = ve.do(V.tensor_tensor(NE, DCUR, DNXT, ALU.not_equal))
        ve.after(t)
        t = ve.do(V.scalar_tensor_tensor(LE, LC, 1.0, NE, ALU.add, ALU.mult))
        ve.after(t)
        t = ve.do(V.tensor_scalar(LE, LE, -1.0, None, ALU.add))
        pe.after(t)
        for n, (v, dst) in enumerate(((LC, LOC), (LE, LOCEND))):
            for h in range(2):
                c0, c1 = (0, 4) if h == 0 else (4, SC)
                for c in range(c0, c1):
                    t = pe.do(T.transpose(bank[2 * n + h][:, (c - c0) * P:(c - c0 + 1) * P], v[:, c * P:(c + 1) * P],
                                          IDENT))
                ve.after(t)
                tables = ve.do(V.tensor_copy(dst[:, c0 * P:c1 * P], bank[2 * n + h][:, 0:(c1 - c0) * P]))

        regs = {e.name: [e.eng.alloc_register(f"{e.name}_base{q}") for q in range(REGS)] for e in (pe, ve)}

        def base(e, n, s, top):
            r = regs[e.name]
            if s % REGS == 0:
                e.after(bases.point)
                e.eng.load(r, BASES[n:n + 1, s:s + REGS])
            return e.eng.snap(r[s % REGS], min_val=0, max_val=top)

        class Steps:
            ADD_LAG = 2
            PAIR = 2

            def __init__(self, regular, locs, cols, banks, tile_ready, acc_ready):
                self.regular, self.locs, self.cols, self.banks = regular, locs, cols, banks
                self.tile_ready, self.acc_ready = tile_ready, acc_ready
                self.product, self.added, self.hot = {}, {}, {}
                self.work, self.last_work, self.group_end = [], 0, {}

            def place(self, s):
                at0 = s % self.PAIR * H2
                return bank[self.banks[s // self.PAIR % len(self.banks)]][:, at0:at0 + self.cols]

            def node_work(self, stages):
                for g in range(NG):
                    room = DONE_BY[g + 1] - DONE_BY[g] if g + 1 < NG else 0
                    pace = max(1, min(4, room // len(stages)))
                    self.work += [(DONE_BY[g] if self.regular else STEPS, pace, stage, g) for stage in stages]

            def run_stage(self):
                _, _, stage, g = self.work.pop(0)
                if g not in self.group_end:
                    for e in (pe, ve, ac):
                        e.after(*self.group_end.get(before_group(g), ()))
                stage(g, self.added[(DONE_BY[g] if self.regular else STEPS) - 1])
                self.group_end[g] = (pe.last, ve.last, ac.last)

            def add(self, s):
                ve.after(self.product[min(s | 1, STEPS - 1)], self.acc_ready, self.added.get(s - 1))
                dst = ACC[:, bass.ds(base(ve, 1, s, (NT - 1) * SLOT), self.cols)]
                self.added[s] = ve.do(V.tensor_tensor(dst, dst, self.place(s), ALU.add))

            def one_hots(self, s):
                n = min(OH_BATCH, STEPS - s)
                ve.after(self.product.get(s + n - 1 - OH_RING))
                self.hot[s // OH_BATCH] = ve.do(V.tensor_tensor(
                    OH[:, s % OH_RING:s % OH_RING + n, :], IOTA.unsqueeze(1).to_broadcast([P, n, P]),
                    self.locs[:, s:s + n].unsqueeze(2).to_broadcast([P, n, P]), ALU.is_equal))

            def step(self, s):
                if s == 0:
                    self.one_hots(0)
                if s % OH_BATCH == 0 and s + OH_BATCH < STEPS:
                    self.one_hots(s + OH_BATCH)
                if s >= self.ADD_LAG:
                    self.add(s - self.ADD_LAG)
                tile = RG[:, bass.ds(base(pe, 0, s, (RING - 1) * SLOT), self.cols)]
                newest = NEWEST[s] if self.regular else min(s, N_ET - 1)
                pe.after(self.hot[s // OH_BATCH], self.added.get((s | 1) - self.PAIR * len(self.banks)),
                         self.tile_ready[newest])
                self.product[s] = pe.do(T.matmul(self.place(s), OH[:, s % OH_RING, :], tile, start=True, stop=True))
                if self.work:
                    ready, pace, _, _ = self.work[0]
                    if s >= ready + self.ADD_LAG and s >= self.last_work + pace:
                        self.last_work = s
                        self.run_stage()

            def finish(self):
                for s in range(STEPS - self.ADD_LAG, STEPS):
                    self.add(s)
                while self.work[0][3] < NG - 2:
                    self.run_stage()
                two = [[w for w in self.work if w[3] == g] for g in (NG - 2, NG - 1)]
                self.work = [w for pair in zip_longest(*two) for w in pair if w]
                while self.work:
                    self.run_stage()

        gtiles = lambda g: range(START[g], START[g + 1])
        gslice = lambda g: slice(START[g], START[g + 1])
        wide = lambda ap, c: ap.rearrange("p (t c) -> p t c", c=c)
        spread = lambda bias, n, c: bias[:, 0:c].unsqueeze(1).to_broadcast([P, n, c])
        xt = lambda j: X[:, j, :]
        at = lambda w: lambda j: ACC3[:, j, 0:w]
        aux = lambda j: AUX3[:, j, :]
        before_group = lambda g: g - 2 if g == NG - 1 else g - 1
        PAIRS = ((4, 5), (6, 7))
        ALL = lambda g: {NG - 2: (4, 5), NG - 1: (6, 7)}.get(g, (4, 5, 6, 7))
        LOW = lambda g: ALL(g)[:len(ALL(g)) // 2]
        HIGH = lambda g: ALL(g)[len(ALL(g)) // 2:]

        def region(buf, g, width, half=0):
            words = GMAX * H2 // (2 if g >= NG - 2 else 1)
            at0 = (words if g == NG - 1 else 0) + half * words // 2
            return buf[:, at0:at0 + GROUPS[g] * width]

        table_rows = lambda t, g, k=1: t.rearrange("(t p k) c -> p t (k c)", p=P, k=k)[:, gslice(g), :]

        def parts(g, per):
            return [(b, q, min(per, GROUPS[g] - q)) for b, q in enumerate(range(0, GROUPS[g], per))]

        def transposes(pt, g, src, width, banks, *before):
            pe.after(*before)
            n = 0
            for j in gtiles(g):
                for b in range(width // P):
                    pt[g] = pe.do(T.transpose(bank[banks[n // 4]][:, (n % 4) * P:(n % 4 + 1) * P],
                                              src(j)[:, b * P:(b + 1) * P], IDENT))
                    n += 1

        def copy_out(pt, g, dst, width, banks, *before):
            ac.after(*before)
            for b, lo in enumerate(range(0, GROUPS[g] * width, 512)):
                m = min(512, GROUPS[g] * width - lo)
                pt[g] = ac.do(A.copy(region(dst, g, width)[:, lo:lo + m], bank[banks[b]][:, 0:m]))

        def copy_out_aux(pt, g, banks, *before):
            ac.after(*before)
            for b, q, n in parts(g, 4):
                j = START[g] + q
                pt[g] = ac.do(A.copy(AUX3[:, j:j + n, :], wide(bank[banks[b]][:, 0:n * P], P)))

        def products(pt, g, lhsT, rhs, width, banks, *before):
            pe.after(*before)
            per = 512 // width
            for q in range(GROUPS[g]):
                left = lhsT(q)
                for k in range(len(rhs)):
                    pt[g] = pe.do(T.matmul(bank[banks[q // per]][:, (q % per) * width:(q % per + 1) * width], left[k], rhs[k],
                                           start=k == 0, stop=k == len(rhs) - 1))

        blocks = lambda buf, g, k=1: lambda q: [region(buf, g, k * P)[:, (k * q + b) * P:(k * q + b + 1) * P] for b in range(k)]

        def layer_norm(src, dst, before, st, sd, iv, nm):
            def stats(g, _):
                ve.after(before[g], iv.get(before_group(g)))
                at0 = GMAX // 2 if g == NG - 1 else 0
                for q, j in enumerate(gtiles(g)):
                    t = ve.do(V.bn_stats(ST[:, at0 + q, :], src(j)))
                ve.after(t)
                for q, j in enumerate(gtiles(g)):
                    st[g] = ve.do(V.bn_aggr(MV[:, j, :], ST[:, at0 + q, :]))

            def deviation(g, _):
                ac.after(st[g], eps_ready)
                sd[g] = ac.do(A.activation(RSTD[:, gslice(g)], MV[:, gslice(g), 1], ACT.Sqrt, bias=eps_col[:]))

            def invert(g, _):
                ve.after(sd[g])
                t = ve.do(V.reciprocal(RSTD[:, gslice(g)], RSTD[:, gslice(g)]))
                ve.after(t)
                iv[g] = ve.do(V.scalar_tensor_tensor(NMR[:, gslice(g)], MV[:, gslice(g), 0], -1.0, RSTD[:, gslice(g)],
                                                     ALU.mult, ALU.mult))

            def normalise(g, _):
                ac.after(iv[g])
                for j in gtiles(g):
                    nm[g] = ac.do(A.activation(dst(j), src(j), ACT.Identity, bias=NMR[:, j:j + 1], scale=RSTD[:, j:j + 1]))
            return [stats, deviation, invert, normalise]

        junk = []

        def norms(which, src, width, before, rn):
            sq, f2, rt = {}, {}, {}

            def squares(g, acc_point):
                ac.after(before(g, acc_point))
                for j in gtiles(g):
                    if len(junk) >= 4:
                        ac.after(junk[-4])
                    sq[g] = ac.do(A.activation(JUNK[:, len(junk) % 4, 0:width], src(j), ACT.Square,
                                               accum_out=SS[:, which, j:j + 1]))
                    junk.append(sq[g])

            def floor(g, _):
                ve.after(sq[g])
                f2[g] = ve.do(V.tensor_scalar(NRM[:, which, gslice(g)], SS[:, which, gslice(g)], NORM_EPS2, None, ALU.max))

            def root(g, _):
                ac.after(f2[g])
                rt[g] = ac.do(A.activation(NRM[:, which, gslice(g)], NRM[:, which, gslice(g)], ACT.Sqrt))

            def inverse(g, _):
                ve.after(rt[g])
                rn[g] = ve.do(V.reciprocal(RN[:, which, gslice(g)], NRM[:, which, gslice(g)]))
            return [squares, floor, root, inverse]

        def h_norm(conv, g):
            t = ve.do(V.tensor_tensor(HN[:, conv, gslice(g)], SS[:, 2, gslice(g)], RN[:, 2, gslice(g)], ALU.mult))
            ve.after(t)
            ve.do(V.tensor_scalar(HN[:, conv, gslice(g)], HN[:, conv, gslice(g)], scal[:, 1 + conv:2 + conv], None, ALU.mult))

        def scale_acc(pt, g, width, conv, before):
            ve.after(before)
            t = ve.do(V.tensor_tensor(RN[:, 0, gslice(g)], RN[:, 0, gslice(g)], HN[:, conv, gslice(g)], ALU.mult))
            ve.after(t)
            for j in gtiles(g):
                pt[g] = ve.do(V.tensor_scalar(ACC3[:, j, 0:width], ACC3[:, j, 0:width], RN[:, 0, j:j + 1], None, ALU.mult))

        class Store:

            def __init__(self, name):
                self.loads = [Loads(sem, f"store_{name}_{k}") for k in range(2)]
                self.pt = {}

            def put(self, g, dst, src, before):
                sp.after(before, self.pt.get(g - 2))
                self.pt[g] = self.loads[g % 2].add(S.dma_start(dst, src))

            @property
            def points(self):
                return [x.point for x in self.loads]

        def normed_rows(pt, g, src, width, table, store, *before):
            ve.after(*before)
            for j in gtiles(g):
                pt[g] = ve.do(V.tensor_scalar(ACC3[:, j, 0:width], src(j), RN[:, 2, j:j + 1], None, ALU.mult))
            store.put(g, table_rows(table, g), ACC3[:, gslice(g), 0:width], pt[g])

        def next_stage(name, *points):
            ends = (pe.last, ve.last, ac.last)
            for e in engines:
                e.after(*ends, *points)
            for e in (pe, ve, ac):
                e.stage(name)

        points = lambda names: [{} for _ in names.split()]

        def gather_pass(steps, table, width, arrived):
            last_use = lambda i: i + LAG
            if steps.regular:
                last_use = lambda i: max(s for s in range(i, min(i + LAG + 1, STEPS)) if OLDEST[s] <= i)

            def load(i):
                if i < N_ET and i not in arrived:
                    po.after(steps.product[last_use(i - RING)] if i >= RING else None, arrived.get(i - AHEAD))
                    arrived[i] = gather(i, table, width)

            for i in range(RING):
                load(i)
            upto = RING
            for s in range(STEPS):
                steps.step(s)
                while upto < N_ET and last_use(upto - RING) <= s:
                    load(upto)
                    upto += 1

        def program(regular):
            next_stage("l0", xload.point, wload.point, tables, src3_stored.point, mask_stored.point, bases.point)
            t = ve.do(V.tensor_scalar(one_eps[:], scal[:, 0:1], 1.0, None, ALU.add))
            ac.after(t)
            for g in range(NG):
                acc0 = ac.do(A.mul(ACC3[:, gslice(g), 0:H], X[:, gslice(g), :], one_eps[:, 0:1]))
                xb2 = ve.do(V.tensor_tensor(AUX3[:, gslice(g), :], X[:, gslice(g), :], spread(b2_0, GROUPS[g], H), ALU.add))
            tr, cp, mm, re, m2, hb, st, sd, iv, nm, ga, s2, d2, i2, n2, rn, tb = points(
                "tr cp mm re m2 hb st sd iv nm ga s2 d2 i2 n2 rn tb")
            store_l1a = Store("l1a")

            def gin_first_product(g, _, mm=mm, cp=cp):
                pe.after(cp[g])
                for b, q, n in parts(g, 4):
                    mm[g] = pe.do(T.matmul(bank[HIGH(g)[b]][:, 0:n * P], w1t0[:], region(ZT, g, P)[:, q * P:(q + n) * P],
                                           start=True, stop=True))

            def relu_bias(mm, re, bias):
                def stage(g, _):
                    ac.after(mm[g])
                    for b, q, n in parts(g, 4):
                        re[g] = ac.do(A.activation(region(HT, g, P)[:, q * P:(q + n) * P], bank[HIGH(g)[b]][:, 0:n * P],
                                                   ACT.Relu, bias=bias[:]))
                return stage

            def gin_residual(g, _, m2=m2, hb=hb):
                ve.after(m2[g], xb2)
                for b, q, n in parts(g, 4):
                    v = AUX3[:, START[g] + q:START[g] + q + n, :]
                    hb[g] = ve.do(V.tensor_tensor(v, wide(bank[LOW(g)[b]][:, 0:n * H], H), v, ALU.add))

            def gin_affine(g, _, nm=nm, ga=ga):
                v = AUX3[:, gslice(g), :]
                ve.after(nm[g])
                t = ve.do(V.tensor_tensor(v, v, spread(gam, GROUPS[g], H), ALU.mult))
                ve.after(t)
                t = ve.do(V.tensor_tensor(v, v, spread(bet, GROUPS[g], H), ALU.add))
                ve.after(t)
                ga[g] = ve.do(V.scalar_tensor_tensor(v, v, 0.0, X[:, gslice(g), :], ALU.max, ALU.add))

            def l1a_table(g, _, rn=rn, tb=tb):
                ve.after(rn[g])
                h_norm(0, g)
                normed_rows(tb, g, xt, H, tab["l1a"], store_l1a)

            arrived = dict(first)
            steps = Steps(regular, LOC, H, (0, 1, 2, 3), arrived, acc0)
            steps.node_work([
                lambda g, acc, tr=tr: transposes(tr, g, at(H), H, LOW(g), acc),
                lambda g, _, tr=tr, cp=cp: copy_out(cp, g, ZT, H, LOW(g), tr[g]),
                gin_first_product,
                relu_bias(mm, re, b1_0),
                lambda g, _, m2=m2, re=re: products(m2, g, blocks(HT, g), [w2t0[:]], H, LOW(g), re[g]),
                gin_residual,
                *layer_norm(aux, aux, hb, st, sd, iv, nm),
                gin_affine,
                *layer_norm(aux, xt, ga, s2, d2, i2, n2),
                *norms(2, xt, H, lambda g, _, n2=n2: n2[g], rn),
                l1a_table])
            gather_pass(steps, tab["l0"], H, arrived)
            steps.finish()

            next_stage("l1a", *store_l1a.points)
            xtr, xcp, rn, sc, tr, cp, mm, ob, io, re, htr, ih, tb, hcp, hm, hb = points(
                "xtr xcp rn sc tr cp mm ob io re htr ih tb hcp hm hb")
            store_l1b, store_hw = Store("l1b"), Store("h1wr1")

            def sage_products(g, _, cp=cp, mm=mm, xcp=xcp):
                products(mm, g, lambda q: blocks(ZT, g)(q) + [aux(START[g] + q)], [wl0[:], wr0[:]], H2, ALL(g), cp[g], xcp[g])

            def sage_bias(g, _, mm=mm, ob=ob):
                ve.after(mm[g])
                for b, q, n in parts(g, 2):
                    j = START[g] + q
                    ob[g] = ve.do(V.tensor_tensor(ACC3[:, j:j + n, 0:H2], wide(bank[ALL(g)[b]][:, 0:n * H2], H2),
                                                  spread(bl0, n, H2), ALU.add))

            def sage_relu(g, _, io=io, re=re):
                ac.after(io[g])
                for j in gtiles(g):
                    re[g] = ac.do(A.activation(ACC3[:, j, 0:H2], ACC3[:, j, 0:H2], ACT.Relu, scale=RN[:, 1, j:j + 1]))

            def l1b_table(g, _, ih=ih, tb=tb, htr=htr):
                ve.after(ih[g])
                h_norm(1, g)
                normed_rows(tb, g, at(H2), H2, tab["l1b"], store_l1b, htr[g])

            def h1_wr1_bias(g, _, hm=hm, hb=hb):
                ve.after(hm[g], store_hw.pt.get(before_group(g)))
                for b, q, n in parts(g, 4):
                    hb[g] = ve.do(V.tensor_tensor(wide(region(HT, g, H)[:, q * H:(q + n) * H], H),
                                                  wide(bank[LOW(g)[b]][:, 0:n * H], H), spread(bl1, n, H), ALU.add))
                store_hw.put(g, table_rows(aux1_dram, g), wide(region(HT, g, H), H), hb[g])

            arrived = {}
            steps = Steps(regular, LOC, H, (0, 1, 2, 3), arrived, None)
            steps.node_work([
                *norms(0, at(H), H, lambda g, acc: acc, rn),
                lambda g, _, sc=sc, rn=rn: scale_acc(sc, g, H, 0, rn[g]),
                lambda g, _, tr=tr, sc=sc: transposes(tr, g, at(H), H, LOW(g), sc[g]),
                lambda g, _, tr=tr, cp=cp: copy_out(cp, g, ZT, H, LOW(g), tr[g]),
                sage_products, sage_bias,
                *norms(1, at(H2), H2, lambda g, _, ob=ob: ob[g], io),
                sage_relu,
                lambda g, _, htr=htr, re=re: transposes(htr, g, at(H2), H2, ALL(g), re[g]),
                *norms(2, at(H2), H2, lambda g, _, re=re: re[g], ih),
                l1b_table,
                lambda g, _, hcp=hcp, htr=htr: copy_out(hcp, g, ZT, H2, ALL(g), htr[g]),
                lambda g, _, hm=hm, hcp=hcp: products(hm, g, blocks(ZT, g, 2), [wr1[:, 0, :], wr1[:, 1, :]], H, LOW(g), hcp[g]),
                h1_wr1_bias])
            for g in range(NG):
                banks = PAIRS[g % 2]
                transposes(xtr, g, xt, H, banks, xcp.get(g - 2))
                copy_out_aux(xcp, g, banks, xtr[g])
            gather_pass(steps, tab["l1a"], H, arrived)
            steps.finish()

            next_stage("l1b", *store_l1b.points, *store_hw.points)
            rn, sc, tr, cp, mm, rl, ob, io, re, st, sd, iv, nm, xtr, xcp, tm, ts = points(
                "rn sc tr cp mm rl ob io re st sd iv nm xtr xcp tm ts")
            store_l2 = Store("l2")
            hw_load = [Loads(sem, f"load_h1wr1_{k}") for k in range(2)]
            R3 = lambda g: wide(region(HT, g, H), H)
            O3 = lambda g: wide(region(HT, g, H, 1), H)
            group_of = lambda j: max(g for g in range(NG) if START[g] <= j)
            r3 = lambda j: R3(group_of(j))[:, j - START[group_of(j)], :]

            def second_load(g, _, rl=rl, nm=nm):
                sp.after(nm.get(before_group(g)), store_l2.pt.get(before_group(g)))
                rl[g] = hw_load[g % 2].add(S.dma_start(R3(g), table_rows(aux1_dram, g)))

            def second_bias(g, _, mm=mm, ob=ob, rl=rl):
                ve.after(mm[g], rl[g])
                for b, q, n in parts(g, 4):
                    rows = R3(g)[:, q:q + n, :]
                    ob[g] = ve.do(V.tensor_tensor(rows, wide(bank[LOW(g)[b]][:, 0:n * H], H), rows, ALU.add))

            def second_residual(g, _, io=io, re=re):
                ve.after(io[g])
                for j in gtiles(g):
                    re[g] = ve.do(V.scalar_tensor_tensor(r3(j), r3(j), RN[:, 1, j:j + 1], xt(j), ALU.mult, ALU.add))

            def message_parts(g, _, tm=tm, ts=ts):
                ve.after(tm[g], store_l2.pt.get(before_group(g)))
                for b, q, n in parts(g, 2):
                    j = START[g] + q
                    both = wide(bank[ALL(g)[b]][:, 0:n * H2], H2)
                    ve.do(V.tensor_tensor(ACC3[:, j:j + n, 0:H], both[:, :, 0:H], spread(bm, n, H), ALU.add))
                    ts[g] = ve.do(V.tensor_copy(O3(g)[:, q:q + n, :], both[:, :, H:H2]))
                store_l2.put(g, table_rows(tab["l2"], g), O3(g), ts[g])

            aux_blocks = lambda g: lambda q: [aux(START[g] + q)]
            arrived = {}
            steps = Steps(regular, LOC, H2, (0, 1, 2, 3), arrived, None)
            steps.node_work([
                *norms(0, at(H2), H2, lambda g, acc: acc, rn),
                lambda g, _, sc=sc, rn=rn: scale_acc(sc, g, H2, 1, rn[g]),
                second_load,
                lambda g, _, tr=tr, sc=sc: transposes(tr, g, at(H2), H2, ALL(g), sc[g]),
                lambda g, _, tr=tr, cp=cp: copy_out(cp, g, ZT, H2, ALL(g), tr[g]),
                lambda g, _, mm=mm, cp=cp: products(mm, g, blocks(ZT, g, 2), [wl1[:, 0, :], wl1[:, 1, :]], H, LOW(g), cp[g]),
                second_bias,
                *norms(1, r3, H, lambda g, _, ob=ob: ob[g], io),
                second_residual,
                *layer_norm(r3, xt, re, st, sd, iv, nm),
                lambda g, _, xtr=xtr, nm=nm: transposes(xtr, g, xt, H, HIGH(g), nm[g]),
                lambda g, _, xtr=xtr, xcp=xcp: copy_out_aux(xcp, g, HIGH(g), xtr[g]),
                lambda g, _, tm=tm, xcp=xcp: products(tm, g, aux_blocks(g), [wms[:, :, :].rearrange("p k h -> p (k h)")], H2,
                                                      ALL(g), xcp[g]),
                message_parts])
            gather_pass(steps, tab["l1b"], H2, arrived)
            steps.finish()

            next_stage("l2", *store_l2.points)
            CH = 4
            NCH = -(-N_ET // CH)
            TURN, BACK = 2, 3
            SCAN = [JUNK[:, 2 * k:2 * k + 2, :].rearrange("p a b -> p (a b)") for k in range(2)]
            acc0 = ve.do(V.memset(ACC3[:, :, H:H + 1], 0.0))
            ones_ready = ve.do(V.memset(RG3[:, :, H:H + 1], 1.0))
            mask_loads = [Loads(sem, f"load_mask_{k}") for k in range(2)]
            arrived, messages, m_ready, turned, scanned, back, loaded = ({} for _ in range(7))
            tiles_of = lambda c: range(c * CH, min((c + 1) * CH, N_ET))
            steps = Steps(regular, LOCEND, H + 1, (0, 1), m_ready, acc0)

            def load_mask(c):
                if c < NCH:
                    sp.after(scanned.get(c - 2))
                    loaded[c] = mask_loads[c % 2].add(S.dma_start(
                        MASK[:, c % 2, :], mask_dram[0:1, c * 512:(c + 1) * 512].to_broadcast([P, 512])))

            def message(i):
                if i < N_ET:
                    ve.after(arrived[i])
                    rows = RG3[:, i % RING, UP:UP + H]
                    messages[i] = ve.do(V.scalar_tensor_tensor(rows, ww[:], WEIGHT[:, i:i + 1], rows, ALU.mult, ALU.add))

            def turn(c):
                pe.after(messages[tiles_of(c)[-1]], scanned.get(c - 1))
                for q, i in enumerate(tiles_of(c)):
                    turned[c] = pe.do(T.transpose(bank[TURN][:, q * P:(q + 1) * P], RG3[:, i % RING, UP:UP + H], IDENT))

            def scan(c):
                n = len(tiles_of(c)) * P
                ve.after(turned[c], loaded[c], back.get(c - 2), scanned.get(c - 1))
                scanned[c] = ve.do(V.tensor_tensor_scan(SCAN[c % 2][:, 0:n], MASK[:, c % 2, 0:n], bank[TURN][:, 0:n],
                                                        SCAN[(c - 1) % 2][:, 511:512] if c else -BIG, ALU.min, ALU.max))

            def turn_back(c):
                n = len(tiles_of(c))
                pe.after(scanned[c], m_ready.get(c * CH - 1))
                for q in range(n):
                    back[c] = pe.do(T.transpose(bank[BACK][:, q * P:(q + 1) * P], SCAN[c % 2][:, q * P:(q + 1) * P], IDENT))
                freeing = c * CH + CH - 1 - AHEAD
                ac.after(back[c], steps.product[freeing] if freeing >= 0 else None, ones_ready)
                slot = (c * CH) % RING
                t = ac.do(A.copy(RG3[:, slot:slot + n, 0:H], wide(bank[BACK][:, 0:n * P], P)))
                for i in tiles_of(c):
                    m_ready[i] = t

            hs, tr, cp, mm, re, m2, ob, st, sd, iv, nm, xtr, xcp, tm, ts = points(
                "hs tr cp mm re m2 ob st sd iv nm xtr xcp tm ts")
            store_l3 = Store("l3")

            def present(g, acc, hs=hs):
                ve.after(acc)
                for j in gtiles(g):
                    hs[g] = ve.do(V.tensor_scalar(at(H)(j), at(H)(j), ACC3[:, j, H:H + 1], None, ALU.mult))

            def max_first_product(g, _, cp=cp, mm=mm):
                pe.after(cp[g])
                for b, q, n in parts(g, 4):
                    o = bank[HIGH(g)[b]][:, 0:n * P]
                    pe.do(T.matmul(o, w1_2[:, 0, :], AUX3[:, START[g] + q:START[g] + q + n, :], start=True, stop=False))
                    mm[g] = pe.do(T.matmul(o, w1_2[:, 1, :], region(ZT, g, P)[:, q * P:(q + n) * P], start=False, stop=True))

            def max_residual(g, _, m2=m2, ob=ob):
                ve.after(m2[g])
                for b, q, n in parts(g, 4):
                    t = ve.do(V.tensor_tensor(ACC3[:, START[g] + q:START[g] + q + n, 0:H], wide(bank[LOW(g)[b]][:, 0:n * H], H),
                                              spread(b2_2, n, H), ALU.add))
                ve.after(t)
                v = ACC3[:, gslice(g), 0:H]
                ob[g] = ve.do(V.tensor_tensor(v, v, X[:, gslice(g), :], ALU.add))

            def l3_table(g, _, tm=tm, ts=ts, m2=m2):
                ve.after(tm[g], m2[g], store_l3.pt.get(before_group(g)))
                o = wide(region(HT, g, H2), H2)
                for b, q, n in parts(g, 2):
                    ts[g] = ve.do(V.tensor_tensor(o[:, q:q + n, :], wide(bank[ALL(g)[b]][:, 0:n * H2], H2),
                                                  spread(bdc, n, H2), ALU.add))
                store_l3.put(g, table_rows(tab["l3"], g, 2), o, ts[g])

            steps.node_work([
                present,
                lambda g, _, tr=tr, hs=hs: transposes(tr, g, at(H), H, LOW(g), hs[g]),
                lambda g, _, tr=tr, cp=cp: copy_out(cp, g, ZT, H, LOW(g), tr[g]),
                max_first_product,
                lambda g, _, mm=mm, re=re: (ac.after(store_l3.pt.get(before_group(g))), relu_bias(mm, re, b1_2)(g, _)),
                lambda g, _, m2=m2, re=re: products(m2, g, blocks(HT, g), [w2_2[:]], H, LOW(g), re[g]),
                max_residual,
                *layer_norm(at(H), xt, ob, st, sd, iv, nm),
                lambda g, _, xtr=xtr, nm=nm: transposes(xtr, g, xt, H, HIGH(g), nm[g]),
                lambda g, _, xtr=xtr, xcp=xcp: copy_out_aux(xcp, g, HIGH(g), xtr[g]),
                lambda g, _, tm=tm, xcp=xcp: products(tm, g, aux_blocks(g), [wdc[:, :, :].rearrange("p k h -> p (k h)")], H2,
                                                      ALL(g), xcp[g]),
                l3_table])
            load_mask(0)
            load_mask(1)
            for i in range(AHEAD):
                arrived[i] = gather(i, tab["l2"], H, UP)
            done = 0

            def steps_before(tile, done, most=STEPS):
                end = min(STEPS, done + most)
                while done < end and (NEWEST[done] if regular else min(done, N_ET - 1)) < tile:
                    steps.step(done)
                    done += 1
                return done

            def ahead(c):
                for i in range(c * CH, min((c + 1) * CH, N_ET)):
                    po.after(messages[i - AHEAD], turned.get((i - RING) // CH))
                    arrived[i] = gather(i, tab["l2"], H, UP)

            for i in range(2 * CH):
                message(i)
            for c in range(AHEAD // CH, AHEAD // CH + 2):
                ahead(c)
            turn(0)
            for c in range(NCH):
                scan(c)
                load_mask(c + 2)
                message((c + 2) * CH)
                done = steps_before(c * CH, done, 1)
                message((c + 2) * CH + 1)
                done = steps_before(c * CH, done, 1)
                if c + 1 < NCH:
                    turn(c + 1)
                message((c + 2) * CH + 2)
                done = steps_before(c * CH, done, 1)
                message((c + 2) * CH + 3)
                turn_back(c)
                ahead(c + 2 + AHEAD // CH)
                done = steps_before(c * CH, done)
            done = steps_before(N_ET, done)
            src3_load = Loads(sem, "load_src3")
            sp.after(*[g.point for g in gathered])
            src3_load.add(S.dma_start(SRC[:], src3_dram))
            steps.finish()

            next_stage("l3", *store_l3.points, src3_load.point)
            sm, sa, re, st, sd, iv, nm = points("sm sa re st sd iv nm")
            store_out = Store("out")
            for g in range(NG):
                banks = PAIRS[g % 2]
                products(sm, g, aux_blocks(g), [wst[:]], H, banks, sa.get(g - 2))
                ve.after(sm[g])
                for b, q, n in parts(g, 4):
                    j = START[g] + q
                    sa[g] = ve.do(V.tensor_tensor(ACC3[:, j:j + n, 0:H], wide(bank[banks[b]][:, 0:n * H], H),
                                                  spread(bs, n, H), ALU.add))

            def relational_residual(g, acc, re=re):
                v = ACC3[:, gslice(g), 0:H]
                ve.after(acc)
                re[g] = ve.do(V.scalar_tensor_tensor(v, v, 0.0, X[:, gslice(g), :], ALU.max, ALU.add))

            def result(g, _, nm=nm):
                full = min(START[g + 1], N // P)
                if full > START[g]:
                    store_out.put(g, out[START[g] * P:full * P, :].rearrange("(t p) c -> p t c", p=P), X[:, START[g]:full, :],
                                  nm[g])
                if full < START[g + 1]:
                    store_out.put(g, out[full * P:N, :], X[0:N % P, NT - 1, :], nm[g])

            arrived = {}
            steps = Steps(regular, LOC, H, (0, 1, 2, 3), arrived, sa[NG - 1])
            steps.node_work([relational_residual, *layer_norm(at(H), xt, re, st, sd, iv, nm), result])
            gather_pass(steps, tab["l3"], H, arrived)
            steps.finish()
            sp.after(*store_out.points)

        for e in engines:
            e.after(flag_ready)
        irregular = nc.values_load(FLAG[0:1, 0:1], min_val=0, max_val=2 * ROWS * P)
        state = [dict(e.waited) for e in engines], [g.count for g in gathered], [e.last for e in engines]

        def restart():
            for e, waited, last in zip(engines, state[0], state[2]):
                e.waited, e.last = dict(waited), last
            for g, count in zip(gathered, state[1]):
                g.count = count
            junk.clear()

        with nc.If(irregular == 0):
            restart()
            program(True)
        with nc.Else():
            restart()
            program(False)


def kernel(**k):
    import concourse.bacc as bacc
    from concourse.bass_utils import run_bass_kernel_spmd as run

    def padded(v, n, fill):
        v = np.asarray(v)
        return np.concatenate([v, np.full((n - v.shape[0],) + v.shape[1:], fill, v.dtype)])

    src, dst = np.asarray(k["src"]), np.asarray(k["dst"])
    tiles = lambda v: padded(v, N_ET * P, 0).reshape(N_ET, P).T
    edge_rows = lambda v: padded(v, ROWS * P, NO_NODE).reshape(ROWS, P)
    consts = np.zeros((P, 3 * P + 3 * SC + 1 + NT), np.float32)
    consts[:, 0:P] = np.eye(P)
    consts[:, P:2 * P] = np.eye(P, k=1)
    consts[:, 2 * P:3 * P] = np.arange(P)
    consts[:, 3 * P:3 * P + SC] = np.arange(SC)[None, :] * P + np.arange(P)[:, None]
    consts[:, 3 * P + SC] = P * (np.arange(P) + 1)
    never = float(2 * ROWS)
    consts[:, 3 * P + SC + 1:3 * P + 2 * SC + 1] = np.array(NEWEST + [never] * (ROWS - STEPS)).reshape(SC, P).T
    consts[:, 3 * P + 2 * SC + 1:3 * P + 3 * SC + 1] = np.array(OLDEST + [-1] * (ROWS - STEPS)).reshape(SC, P).T
    consts[:, 3 * P + 3 * SC + 1:] = [DONE_BY[START.index(t + 1) - 1] if t + 1 in START else never for t in range(NT)]
    r = lambda name: np.asarray(k[name]).reshape(1, -1)
    arrays = {
        "x": padded(k["x"], NP, 0), "src_cols": tiles(src), "type_cols": tiles(k["edge_type_2"]),
        "dst_rows": edge_rows(dst), "next_rows": edge_rows(dst[1:]),
        "prev_rows": edge_rows(np.concatenate([np.full(1, NO_NODE, dst.dtype), dst])),
        "weight_cols": tiles(k["edge_weight"]), "consts": consts,
        "l0_w1t": k["L0_gnn_W1"].T, "l0_w2t": k["L0_gnn_W2"].T, "l0_b1": r("L0_gnn_b1"), "l0_b2": r("L0_gnn_b2"),
        "l0_gamma": r("L0_gnn_gamma"), "l0_beta": r("L0_gnn_beta"), "l0_eps": r("L0_gnn_eps"),
        "l1_scale0": r("L1_gnn_scale0"), "l1_scale1": r("L1_gnn_scale1"),
        "l1_wl0": k["L1_gnn_Wl0"], "l1_wr0": k["L1_gnn_Wr0"], "l1_wl1": k["L1_gnn_Wl1"], "l1_wr1": k["L1_gnn_Wr1"],
        "l1_bl0": r("L1_gnn_bl0"), "l1_bl1": r("L1_gnn_bl1"),
        "l2_wm": k["L2_gnn_Wm"], "l2_bm": r("L2_gnn_bm"), "l2_w1": k["L2_gnn_W1"], "l2_b1": r("L2_gnn_b1"),
        "l2_w2": k["L2_gnn_W2"], "l2_b2": r("L2_gnn_b2"),
        "l3_wdt": k["L3_gnn_W_data"].T, "l3_wct": k["L3_gnn_W_control"].T, "l3_wst": k["L3_gnn_W_self"].T,
        "l3_bd": r("L3_gnn_b_data"), "l3_bc": r("L3_gnn_b_control"), "l3_bs": r("L3_gnn_b_self"),
    }
    arrays = {n: np.ascontiguousarray(v) for n, v in arrays.items()}
    nc = bacc.Bacc("TRN2", target_bir_lowering=False, num_devices=1)
    a = {n: nc.dram_tensor(f"in_{n}", v.shape, mybir.dt.from_np(v.dtype), kind="ExternalInput").ap() for n, v in arrays.items()}
    out = nc.dram_tensor("out", (N, H), F32, kind="ExternalOutput").ap()
    build(nc, a, out)
    return run(nc, [{f"in_{n}": v for n, v in arrays.items()}], core_ids=[0]).results[0]["out"]
```
